# Optimizing a Trainium2 kernel written in Bass

```python
import numpy as np
import jax
import jax.numpy as jnp

def _softmax(x, axis=-1):
    return jax.nn.softmax(x, axis=axis)

def _gelu(x):
    return jax.nn.gelu(x, approximate=True)

def _silu(x):
    return jax.nn.silu(x)

def _sigmoid(x):
    return jax.nn.sigmoid(x)

def _layernorm(x, axis=-1, eps=1e-05):
    m = jnp.mean(x, axis=axis, keepdims=True)
    v = jnp.var(x, axis=axis, keepdims=True)
    return (x - m) / jnp.sqrt(v + eps)

def _scatter_add(tgt, idx, src, axis=0):
    return tgt.at[idx].add(src)

def _segment_sum(src, seg, n):
    return jax.ops.segment_sum(src, seg, n)
kernel_name = 'mk_seq_postln_d1_jaxref_r8_72d564'

def setup_inputs(seed: int=0):
    np.random.seed(seed)
    _w = jnp.asarray

    def _L0_attn_setup():
        import jax, jax.numpy as jnp
        import numpy as np
        EMBED_DIM = 256
        NUM_HEADS = 16
        HEAD_DIM = EMBED_DIM // NUM_HEADS
        BASE = 10000.0

        def rotate_half(x):
            half = x.shape[-1] // 2
            x1, x2 = (x[..., :half], x[..., half:])
            return jnp.concatenate([-x2, x1], axis=-1)

        def apply_rope(x, base=BASE):
            S, Dh = (x.shape[-2], x.shape[-1])
            inv_freq = 1.0 / base ** (jnp.arange(0, Dh, 2, dtype=jnp.float32) / Dh)
            t = jnp.arange(S, dtype=jnp.float32)
            freqs = jnp.einsum('i,j->ij', t, inv_freq)
            emb = jnp.concatenate([freqs, freqs], axis=-1)
            return x * jnp.cos(emb) + rotate_half(x) * jnp.sin(emb)
        key = jax.random.key(seed)
        ks = jax.random.split(key, 9)
        B, S, D = (2, 256, EMBED_DIM)
        xavier = lambda k, shape: jax.random.uniform(k, shape, jnp.float32, -1.0, 1.0) * float(np.sqrt(6.0 / (shape[0] + shape[1])))
        return {'x': jax.random.normal(ks[0], (B, S, D), jnp.float32), 'q_w': xavier(ks[1], (D, D)), 'k_w': xavier(ks[2], (D, D)), 'v_w': xavier(ks[3], (D, D)), 'q_b': jnp.zeros((D,), jnp.float32), 'k_b': jnp.zeros((D,), jnp.float32), 'v_b': jnp.zeros((D,), jnp.float32), 'out_w': xavier(ks[4], (D, D)), 'out_b': jnp.zeros((D,), jnp.float32)}
    _L0_attn_in = _L0_attn_setup()

    def _L0_ffn_setup():
        import jax, jax.numpy as jnp
        import numpy as np
        B, S, H, E, I, TOPK = (1, 128, 256, 16, 128, 2)
        SCALE = 1.0
        key = jax.random.key(seed)
        k0, k1, k2, k3 = jax.random.split(key, 4)
        hidden_states = jax.random.normal(k0, (B, S, H), dtype=jnp.float32)
        gate_w = jax.random.normal(k1, (E, H), dtype=jnp.float32) * 0.02
        gate_up_proj = jax.random.normal(k2, (E, H, 2 * I), dtype=jnp.float32) / np.sqrt(H)
        down_proj = jax.random.normal(k3, (E, I, H), dtype=jnp.float32) / np.sqrt(I)
        return {'hidden_states': hidden_states, 'gate_w': gate_w, 'gate_up_proj': gate_up_proj, 'down_proj': down_proj}
    _L0_ffn_in = _L0_ffn_setup()
    _d = {'L0_attn_x': _L0_attn_in['x'], 'L0_attn_q_w': _L0_attn_in['q_w'], 'L0_attn_k_w': _L0_attn_in['k_w'], 'L0_attn_v_w': _L0_attn_in['v_w'], 'L0_attn_q_b': _L0_attn_in['q_b'], 'L0_attn_k_b': _L0_attn_in['k_b'], 'L0_attn_v_b': _L0_attn_in['v_b'], 'L0_attn_out_w': _L0_attn_in['out_w'], 'L0_attn_out_b': _L0_attn_in['out_b'], 'L0_ffn_gate_w': _L0_ffn_in['gate_w'], 'L0_ffn_gate_up_proj': _L0_ffn_in['gate_up_proj'], 'L0_ffn_down_proj': _L0_ffn_in['down_proj']}
    _x0 = _d['L0_attn_x']
    _d['L0_attn_x'] = jax.random.normal(jax.random.fold_in(jax.random.key(seed), 1), (16, 256, 256), dtype=_x0.dtype)
    del _x0
    return _d

def reference(L0_attn_x, L0_attn_q_w, L0_attn_k_w, L0_attn_v_w, L0_attn_q_b, L0_attn_k_b, L0_attn_v_b, L0_attn_out_w, L0_attn_out_b, L0_ffn_gate_w, L0_ffn_gate_up_proj, L0_ffn_down_proj):

    def _L0_attn_ref(x, q_w, k_w, v_w, q_b, k_b, v_b, out_w, out_b):
        import jax, jax.numpy as jnp
        import numpy as np
        EMBED_DIM = 256
        NUM_HEADS = 16
        HEAD_DIM = EMBED_DIM // NUM_HEADS
        BASE = 10000.0

        def rotate_half(x):
            half = x.shape[-1] // 2
            x1, x2 = (x[..., :half], x[..., half:])
            return jnp.concatenate([-x2, x1], axis=-1)

        def apply_rope(x, base=BASE):
            S, Dh = (x.shape[-2], x.shape[-1])
            inv_freq = 1.0 / base ** (jnp.arange(0, Dh, 2, dtype=jnp.float32) / Dh)
            t = jnp.arange(S, dtype=jnp.float32)
            freqs = jnp.einsum('i,j->ij', t, inv_freq)
            emb = jnp.concatenate([freqs, freqs], axis=-1)
            return x * jnp.cos(emb) + rotate_half(x) * jnp.sin(emb)
        B, S, D = x.shape
        H, Dh = (NUM_HEADS, HEAD_DIM)
        scaling = Dh ** (-0.5)
        q = (x @ q_w.T + q_b).reshape(B, S, H, Dh).transpose(0, 2, 1, 3)
        k = (x @ k_w.T + k_b).reshape(B, S, H, Dh).transpose(0, 2, 1, 3)
        v = (x @ v_w.T + v_b).reshape(B, S, H, Dh).transpose(0, 2, 1, 3)
        q = apply_rope(q)
        k = apply_rope(k)
        attn = jnp.einsum('bhqd,bhkd->bhqk', q, k) * scaling
        probs = jax.nn.softmax(attn, axis=-1)
        out = jnp.einsum('bhqk,bhkd->bhqd', probs, v)
        out = out.transpose(0, 2, 1, 3).reshape(B, S, D)
        return out @ out_w.T + out_b

    def _L0_ffn_ref(hidden_states, gate_w, gate_up_proj, down_proj):
        import jax, jax.numpy as jnp
        import numpy as np
        B, S, H, E, I, TOPK = (1, 128, 256, 16, 128, 2)
        SCALE = 1.0
        b, s, h = hidden_states.shape
        e = gate_w.shape[0]
        x = hidden_states.reshape(-1, h)
        logits = jnp.matmul(x.astype(jnp.float32), gate_w.T.astype(jnp.float32))
        p = jax.nn.sigmoid(logits)
        p = p / jnp.sum(p, axis=-1, keepdims=True)
        w, idx = jax.lax.top_k(p, TOPK)
        w = w / jnp.sum(w, axis=-1, keepdims=True)
        w = w * SCALE
        combine = jnp.sum(jax.nn.one_hot(idx, e, dtype=w.dtype) * w[..., None], axis=1)
        gu = jnp.einsum('th,ehf->etf', x, gate_up_proj)
        gate, up = jnp.split(gu, 2, axis=-1)
        inter = jax.nn.silu(gate) * up
        y = jnp.einsum('eti,eih->eth', inter, down_proj)
        out = jnp.einsum('eth,te->th', y, combine.astype(y.dtype))
        return out.reshape(b, s, h)
    x = L0_attn_x
    x = _layernorm(x + _L0_attn_ref(x, L0_attn_q_w, L0_attn_k_w, L0_attn_v_w, L0_attn_q_b, L0_attn_k_b, L0_attn_v_b, L0_attn_out_w, L0_attn_out_b), axis=-1)
    x = _layernorm(x + _L0_ffn_ref(x, L0_ffn_gate_w, L0_ffn_gate_up_proj, L0_ffn_down_proj), axis=-1)
    return x

_drawn_inputs = setup_inputs


def setup_inputs(seed=0):
    import zlib

    import numpy as np

    out = dict(_drawn_inputs(seed))
    spreads = {'L0_attn_q_b': (0.0, 0.1),
     'L0_attn_k_b': (0.0, 0.1),
     'L0_attn_v_b': (0.0, 0.1),
     'L0_attn_out_b': (0.0, 0.1)}
    factors = {}
    for name, (base, spread) in spreads.items():
        noise = np.random.default_rng([zlib.crc32(name.encode()), seed]).standard_normal(out[name].shape)
        drawn = base * np.exp(spread * noise) if base else spread * noise
        out[name] = jnp.asarray(drawn.astype(out[name].dtype))
    for name, factor in factors.items():
        out[name] = (out[name] * factor).astype(out[name].dtype)
    return out
```

```python
from contextlib import ExitStack

import concourse.bass as bass
import numpy as np
from concourse import mybir

ALU = mybir.AluOpType
ACT = mybir.ActivationFunctionType
AX = mybir.AxisListType
F32 = mybir.dt.float32
BF16 = mybir.dt.bfloat16
F16 = mybir.dt.float16
I32 = mybir.dt.int32

P = 128
B, S, D = 16, 256, 256
H, DH = 16, 16
E, I, TOPK = 16, 128, 2
TOK = B * S
TILES = TOK // P
KC = D // P
ST = S // P
EPS = 1e-5
SCALE = float(DH) ** -0.5
NBLK = (TOK * TOPK + E * (P - 1)) // P
NBLK += NBLK % 2
ID0 = TOK // 2
QROWS = 6 * DH
SROWS = QROWS + 2

CONST = {}
_at = 0
for _name, _n in (("ident", P), ("before", P), ("cos", ST * P), ("sin", ST * P), ("rev", E), ("full", TILES),
                  ("lower", E * E), ("iota", P), ("blocks", NBLK), ("token", TILES)):
    CONST[_name] = (_at, _at + _n)
    _at += _n
NCONST = _at

UNITS = [
    (0, "pv0", 3), (0, "qk0", 0), (0, "mt3", 3), (0, "tp0", 1),
    (1, "tp1", 1), (1, "tp2", 1),
    (2, "pv1", 3), (2, "qk1", 0), (2, "mt0", 2),
    (3, "vv", 2), (3, "tr0", 4), (3, "tr1", 4),
    (4, "pv2", 3), (4, "mt1", 2), (4, "at", 4),
    (5, "op", 4), (5, "xt", 5),
    (6, "pv3", 3), (6, "mt2", 2),
    (7, "lg", 5),
]
NAMES = [u[1] for u in UNITS]
LAG = {u[1]: u[2] for u in UNITS}
BANK = {name: n % 2 for n, name in enumerate(NAMES)}
MAXLAG = 5
LOOP_FROM, LOOP_TO, ITERATIONS = 6, B - 2, B + MAXLAG


def runs(i, lag):
    return not isinstance(i, int) or 0 <= i - lag < B


def iterations(engine, body):
    for i in range(LOOP_FROM):
        body(i, i % 2)
    with engine.Fori(0, (LOOP_TO - LOOP_FROM) // 2) as trip:
        for u in range(2):
            body(2 * trip + (LOOP_FROM + u), u)
    for i in range(LOOP_TO, ITERATIONS):
        body(i, i % 2)


def build(nc, x, xT, wqkT, wvT, woT, gateT, bqk, bv, bo, gup, down, const, out):
    x_t = x.rearrange("(t p) d -> p t d", p=P)
    out_t = out.rearrange("(t p) d -> p t d", p=P)
    xT_c = xT.rearrange("(c p) t -> p c t", p=P)

    planes_dram = nc.dram_tensor("planes_dram", (2, 4 * 3, P, S), BF16).ap()
    x1_dram = nc.dram_tensor("x1_dram", (TOK, D), F32).ap()
    ys_dram = nc.dram_tensor("ys_dram", (NBLK * P, D), F32).ap()
    x1_t = x1_dram.rearrange("(t p) d -> p t d", p=P)
    ys_t = ys_dram.rearrange("(b p) d -> p b d", p=P)

    with ExitStack() as ctx:
        def sb(name, shape, dt=F32):
            return ctx.enter_context(nc.sbuf_tensor(name, shape, dt))

        def sem(name):
            return ctx.enter_context(nc.semaphore(name))

        cst = sb("cst", [P, NCONST])
        def c(name):
            a, b = CONST[name]
            return cst[:, a:b]
        ident16 = sb("ident16", [P, P], BF16)
        before16 = sb("before16", [P, P], BF16)
        ones16 = sb("ones16", [P, P], BF16)
        iota16 = sb("iota16", [P, P], F16)
        blocks16 = sb("blocks16", [P, NBLK], F16)
        half_neg = sb("half_neg", [P, 2])
        wqk = sb("wqk", [P, KC, 2 * D])
        wv = sb("wv", [P, KC, D])
        wo = sb("wo", [P, KC, D])
        gw = sb("gw", [P, KC, E])
        bqk_sb = sb("bqk_sb", [P, 2 * D])
        bv_sb = sb("bv_sb", [P, D])
        bo_sb = sb("bo_sb", [P, D])

        xT_qk = sb("xT_qk", [P, 2, KC, S])
        xT_v = sb("xT_v", [P, 2, KC, S])
        xn = sb("xn", [P, 2, ST, D])
        xb = sb("xb", [P, ST, D])
        qk = sb("qk", [P, ST, 2 * D])
        rope_a = sb("rope_a", [P, 2 * D])
        rope_b = sb("rope_b", [P, 2 * D])
        planes = sb("planes", [P, 2, ST, 3, 2 * D], BF16)
        planesT = sb("planesT", [P, 4, 3, S], BF16)
        stacks = sb("stacks", [P, 2, 2, 2, 8, S], BF16)
        V = sb("V", [P, 2, ST, H, 32])
        negmax = sb("negmax", [P, ST, H])
        mplanes = sb("mplanes", [P, 4, ST, 2, 4], BF16)
        mT = sb("mT", [8, 4, S], BF16)
        probs = sb("probs", [P, 4, 4, S])
        outT = sb("outT", [P, 2, 4, S])
        inv = sb("inv", [P, ST, H])
        attn = sb("attn", [P, ST, D])
        attnT = sb("attnT", [P, KC, S])
        y = sb("y", [P, ST, D])
        stats = sb("stats", [P, ST, 6])
        moments = sb("moments", [P, ST, 2])
        vareps = sb("vareps", [P, ST])
        rstd = sb("rstd", [P, ST])
        x1 = sb("x1", [P, 2, ST, D])
        x1T = sb("x1T", [P, KC, S])
        logits = sb("logits", [P, TILES, E])

        wgu = sb("wgu", [P, KC, E, 2 * I])
        late = stacks[:].rearrange("p a b c h t -> p (a b c h t)").bitcast(F32)
        wdn = late[:, 0:E * D].rearrange("p (e h) -> p e h", e=E)
        y_top = late[:, E * D:E * D + 8 * D].rearrange("p (a k h) -> p a k h", a=4, k=TOPK)
        x1b = late[:, E * D + 8 * D:E * D + 12 * D].rearrange("p (a h) -> p a h", a=4)
        probs_f = probs[:].rearrange("p a b s -> p (a b s)")
        R = TILES * E
        r_p = probs_f[:, 0:R].rearrange("p (t e) -> p t e", e=E)
        r_a = probs_f[:, R:2 * R].rearrange("p (t e) -> p t e", e=E)
        r_b = probs_f[:, 2 * R:3 * R].rearrange("p (t e) -> p t e", e=E)
        r_oh = [probs_f[:, (3 + k) * R:(4 + k) * R].rearrange("p (t e) -> p t e", e=E) for k in range(2)]
        r_big = probs_f[:, 5 * R:5 * R + NBLK * E]
        col = sb("col", [P, 8, TILES])
        w_top = sb("w_top", [P, 2, TILES])
        chosen16 = sb("chosen16", [P, TILES, E], BF16)
        counts = sb("counts", [P, 4, E])
        slot_f = sb("slot_f", [P, 2, TILES])
        slot_i = sb("slot_i", [P, 2, TILES], I32)
        part_i = sb("part_i", [P, 2, 2, TILES], I32)
        part_f = sb("part_f", [P, 2, 2, TILES])
        oh_in = sb("oh_in", [P, 4, P], F16)
        oh_blk = sb("oh_blk", [P, 4, NBLK], F16)
        ids_f = sb("ids_f", [P, NBLK])
        ids_i = sb("ids_i", [P, NBLK], I32)
        be_f = sb("be_f", [1, NBLK])
        be_i = sb("be_i", [1, NBLK], I32)
        id_cur = sb("id_cur", [P, 4], I32)
        xg = sb("xg", [P, 4, D])
        xgT = sb("xgT", [P, 2, KC, P])
        expg = sb("expg", [P, 2, I])
        den = sb("den", [P, I])
        rec = sb("rec", [P, I])
        sg = sb("sg", [P, I])
        inter = sb("inter", [P, 2, I])
        interT = sb("interT", [P, 2, P])
        yb = sb("yb", [P, 4, D])
        slot_cur = sb("slot_cur", [P, 4, 2], I32)
        z = sb("z", [P, 4, D])
        z_stats = sb("z_stats", [P, 4, 6])
        z_moments = sb("z_moments", [P, 4, 2])
        z_var = sb("z_var", [P, 4])
        z_rs = sb("z_rs", [P, 4])
        o = sb("o", [P, 4, D])

        ps_score = ctx.enter_context(nc.psum_tensor("ps_score", [P, 2, 4, S], F32))
        ps_max = ctx.enter_context(nc.psum_tensor("ps_max", [P, 2, ST, S], F32))
        ps_unit = ctx.enter_context(nc.psum_tensor("ps_unit", [P, 2, 512], F32))

        s_const, s_wqk, s_w, s_experts = (sem("const_loaded"), sem("qk_weights_loaded"), sem("weights_loaded"),
                                          sem("experts_loaded"))
        s_setup, s_setup_pool = sem("setup_vector"), sem("setup_pool")
        s_xqk = [sem(f"xT_qk_loaded{u}") for u in range(2)]
        s_xv = [sem(f"xT_v_loaded{u}") for u in range(2)]
        s_xn = [sem(f"xn_loaded{u}") for u in range(2)]
        s_planes_out = sem("planes_written")
        s_stack = [sem(f"stack_half_loaded{u}") for u in range(2)]
        s_mrows = [sem(f"max_rows_loaded{g}") for g in range(4)]
        s_x1_out = sem("x1_written")
        filled = {n: sem(f"filled_{n}") for n in NAMES}
        emptied = {n: sem(f"emptied_{n}") for n in NAMES}
        s_score, s_exp = sem("score_pair_filled"), sem("exp_pair_done")
        s_max, s_red = sem("max_head_filled"), sem("max_head_reduced")
        s_mhi, s_mpl = sem("max_high_plane"), sem("max_planes_done")
        s_rope = sem("rope_step")
        s_xb, s_inv = sem("x_with_bias"), sem("sums_inverted")
        s_stats, s_mom, s_ve, s_rstd, s_x1 = (sem("ln_stats"), sem("ln_moments"), sem("ln_var_eps"),
                                             sem("ln_rstd"), sem("x1_done"))
        s_rexp, s_r = sem("router_exp"), sem("router_step")
        s_pos = sem("positions_filled")
        s_oh, s_ohu = sem("one_hots_done"), sem("one_hots_used")
        s_route = sem("routing_done")
        s_idc, s_xg = sem("block_ids_copied"), [sem(f"rows_gathered{u}") for u in range(4)]
        s_xt, s_xte = sem("block_xT_filled"), sem("block_xT_emptied")
        s_gu, s_ge, s_den, s_rec, s_sg, s_in = (sem("gate_up_filled"), sem("gate_exp_done"), sem("gate_den_done"),
                                                sem("gate_rec_done"), sem("gate_silu_done"), sem("inter_done"))
        s_it, s_ite = sem("interT_filled"), sem("interT_emptied")
        s_y, s_ye = sem("block_y_filled"), sem("block_y_emptied")
        s_ys = [sem(f"block_y_written{u}") for u in range(4)]
        s_slc, s_yt = sem("slots_copied"), [sem(f"y_gathered{u}") for u in range(4)]
        s_x1b = [sem(f"x1_reloaded{u}") for u in range(4)]
        s_z, s_zs, s_zm, s_zv, s_zr, s_o = (sem("z_step"), sem("z_stats"), sem("z_moments"), sem("z_var_eps"),
                                            sem("z_rstd"), sem("out_done"))
        s_out = [sem(f"out_written{u}") for u in range(4)]

        def unit(name, dt=F32):
            bank = ps_unit[:, BANK[name], :]
            return bank if dt == F32 else bank.bitcast(dt)

        def wait_bank(pe, i, name):
            n = NAMES.index(name)
            for back in range(1, len(UNITS) * (MAXLAG + 2)):
                m = n - back
                turn = i + (m // len(UNITS))
                other = NAMES[m % len(UNITS)]
                if BANK[other] == BANK[name] and runs(turn, LAG[other]):
                    if isinstance(turn, int) and turn < 0:
                        return
                    pe.wait_ge(emptied[other], turn - LAG[other] + 1)
                    return

        def is_filled(engine, i, name):
            engine.wait_ge(filled[name], i - LAG[name] + 1)

        def was_emptied(engine, i, name):
            engine.wait_ge(emptied[name], i - LAG[name] + 1)

        def apart(engine):
            engine.nop(nofuse=True)

        N_W_DMA = 5
        STACK_DMAS = 9
        X = AX.X

        block = ctx.enter_context(nc.Block())

        @block.sync
        def _(sp):
            sp.dma_start(xT_qk[:, 0], xT_c[:, :, 0:S]).then_inc(s_xqk[0], 16)
            sp.dma_start(wqk[:], wqkT.rearrange("(c p) n -> p c n", p=P)).then_inc(s_wqk, 16)
            sp.dma_start(bqk_sb[:], bqk).then_inc(s_wqk, 16)
            sp.dma_start(cst[:], const).then_inc(s_const, 16)
            for dst, src in ((wv[:], wvT.rearrange("(c p) n -> p c n", p=P)),
                             (wo[:], woT.rearrange("(c p) n -> p c n", p=P)),
                             (gw[:], gateT.rearrange("(c p) n -> p c n", p=P)), (bv_sb[:], bv), (bo_sb[:], bo)):
                sp.dma_start(dst, src).then_inc(s_w, 16)

            def max_rows(i, g, lag, u):
                was_emptied(sp, i, f"mt{g}")
                dst = stacks[QROWS:SROWS, u, 0, g // 2, 4 * (g % 2):4 * (g % 2) + 4, :]
                sp.dma_start(dst, mT[:, g, :]).then_inc(s_mrows[g], 16)

            def stack_half(b, u, hh):
                rows = planes_dram[u].rearrange("(c l) (d h) t -> c (l d) (h t)", l=3, h=8)
                at = 0
                for plane in range(3):
                    n = (3 - plane) * DH
                    sp.dma_start(stacks[at:at + n, u, 0, hh].rearrange("p h t -> p (h t)"),
                                 rows[hh, 0:n, :]).then_inc(s_stack[hh], 16)
                    for r in range(3 - plane):
                        sp.dma_start(stacks[at + r * DH:at + (r + 1) * DH, u, 1, hh].rearrange("p h t -> p (h t)"),
                                     rows[2 + hh, plane * DH:(plane + 1) * DH, :]).then_inc(s_stack[hh], 16)
                    at += n

            def body(i, u):
                if runs(i, 3):
                    max_rows(i, 3, 3, 1 - u)
                if runs(i + 1, 0):
                    if not isinstance(i, int) or i >= 1:
                        sp.wait_ge(filled["qk1"], i)
                    sp.dma_start(xT_qk[:, 1 - u], xT_c[:, :, bass.ds((i + 1) * S, S)]).then_inc(s_xqk[1 - u], 16)
                if runs(i, 1):
                    if not isinstance(i, int) or i >= 3:
                        sp.wait_ge(filled["vv"], i - 2)
                    sp.dma_start(xT_v[:, 1 - u], xT_c[:, :, bass.ds((i - 1) * S, S)]).then_inc(s_xv[1 - u], 16)
                if runs(i, 3):
                    if not isinstance(i, int) or i >= 5:
                        sp.wait_ge(s_xb, i - 4)
                    sp.dma_start(xn[:, 1 - u], x_t[:, bass.ds((i - 3) * ST, ST), :]).then_inc(s_xn[1 - u], 16)
                if runs(i, 1):
                    was_emptied(sp, i, "tp0")
                    was_emptied(sp, i, "tp1")
                    was_emptied(sp, i, "tp2")
                    sp.dma_start(planes_dram[1 - u].rearrange("c p t -> p c t"),
                                 planesT[:].rearrange("p c l t -> p (c l) t")).then_inc(s_planes_out, 16)
                if runs(i, 2):
                    max_rows(i, 0, 2, u)
                if runs(i, 1):
                    sp.wait_ge(s_planes_out, 16 * (i - 1) + 16)
                    if runs(i, 3):
                        sp.wait_ge(s_score, 8 * (i - 3) + 4)
                    stack_half(i - 1, 1 - u, 0)
                if runs(i, 2):
                    max_rows(i, 1, 2, u)
                if runs(i, 1):
                    if runs(i, 3):
                        sp.wait_ge(s_score, 8 * (i - 3) + 8)
                    stack_half(i - 1, 1 - u, 1)
                if runs(i, 2):
                    max_rows(i, 2, 2, u)
                if runs(i, 4):
                    sp.wait_ge(s_x1, ST * (i - 4) + ST)
                    sp.dma_start(x1_t[:, bass.ds((i - 4) * ST, ST), :], x1[:, u]).then_inc(s_x1_out, 16)
                if isinstance(i, int) and i == 2:
                    for chunk in range(KC):
                        sp.dma_start(wgu[:, chunk], gup[:, chunk * P:(chunk + 1) * P, :].rearrange("e p f -> p e f")
                                     ).then_inc(s_experts, 16)
                if isinstance(i, int) and i == B + 2:
                    sp.wait_ge(s_score, 8 * B)
                    sp.dma_start(wdn, down.rearrange("e p h -> p e h")).then_inc(s_experts, 16)

            iterations(sp, body)

            with sp.Fori(0, NBLK // 4) as trip:
                for u in range(4):
                    b = 4 * trip + u
                    sp.wait_ge(s_ye, b + 1)
                    sp.dma_start(ys_t[:, bass.ds(b, 1), :], yb[:, u:u + 1, :]).then_inc(s_ys[u], 16)
            def reload(t, u):
                sp.dma_start(x1b[:, u:u + 1, :], x1_t[:, bass.ds(t, 1), :]).then_inc(s_x1b[u], 16)
            for u in range(4):
                reload(u, u)
            with sp.Fori(0, TILES // 4 - 1) as trip:
                for u in range(4):
                    t = 4 * trip + u
                    sp.wait_ge(s_o, t + 1)
                    sp.dma_start(out_t[:, bass.ds(t, 1), :], o[:, u:u + 1, :]).then_inc(s_out[u], 16)
                    reload(t + 4, u)
            for u in range(4):
                t = TILES - 4 + u
                sp.wait_ge(s_o, t + 1)
                sp.dma_start(out_t[:, t:t + 1, :], o[:, u:u + 1, :]).then_inc(s_out[u], 16)
            for u in range(4):
                sp.wait_ge(s_out[u], 16 * TILES // 4)

        @block.gpsimd
        def _(pool):
            pool.memset(half_neg[:], -0.5).then_inc(s_setup_pool, 1)
            pool.memset(V[:], 0.0).then_inc(s_setup_pool, 1)
            pool.wait_ge(s_setup_pool, 2)
            pool.memset(V[:, :, :, :, DH:DH + 1], 1.0).then_inc(s_setup_pool, 1)
            pool.wait_ge(s_const, 16)
            pool.wait_ge(s_w, 16 * N_W_DMA)

            def rope(i, u, t):
                n = 16 * i + 8 * t
                cos = c("cos")[:, t * P:(t + 1) * P].unsqueeze(1).to_broadcast([P, 4, P])
                sin = c("sin")[:, t * P:(t + 1) * P]
                q4 = qk[:, t].rearrange("p (c n) -> p c n", c=4)
                a4 = rope_a[:].rearrange("p (c n) -> p c n", c=4)
                b4 = rope_b[:].rearrange("p (c n) -> p c n", c=4)
                h = P // 2
                if not isinstance(i, int) or n > 0:
                    pool.wait_ge(s_rope, n)
                pool.wait_ge(emptied[f"qk{t}"], i + 1)
                pool.tensor_tensor(a4, q4, cos, ALU.mult).then_inc(s_rope, 1)
                for lo, other in ((0, h), (h, 0)):
                    pool.tensor_tensor(b4[:, :, lo:lo + h], q4[:, :, other:other + h],
                                       sin[:, lo:lo + h].unsqueeze(1).to_broadcast([P, 4, h]),
                                       ALU.mult).then_inc(s_rope, 1)
                pool.wait_ge(s_rope, n + 3)
                pool.tensor_tensor(rope_a[:], rope_a[:], rope_b[:], ALU.add).then_inc(s_rope, 1)
                if not isinstance(i, int) or i >= 2:
                    pool.wait_ge(filled["tp2"], i - 1)
                pool.wait_ge(s_rope, n + 4)
                apart(pool)
                pool.tensor_scalar(planes[:, u, t, 0], rope_a[:], 1.0, 0.0, ALU.mult, ALU.add).then_inc(s_rope, 1)
                pool.wait_ge(s_rope, n + 5)
                pool.tensor_tensor(rope_b[:], rope_a[:], planes[:, u, t, 0], ALU.subtract).then_inc(s_rope, 1)
                pool.wait_ge(s_rope, n + 6)
                apart(pool)
                pool.tensor_scalar(planes[:, u, t, 1], rope_b[:], 1.0, 0.0, ALU.mult, ALU.add).then_inc(s_rope, 1)
                pool.wait_ge(s_rope, n + 7)
                pool.tensor_tensor(planes[:, u, t, 2], rope_b[:], planes[:, u, t, 1], ALU.subtract).then_inc(s_rope, 1)

            def body(i, u):
                if runs(i, 4):
                    b = i - 4
                    pool.wait_ge(s_xn[u], 8 * (b - u) + 16)
                    if not isinstance(i, int) or i >= 5:
                        pool.wait_ge(emptied["op"], b)
                    pool.tensor_tensor(xb[:], xn[:, u], bo_sb[:].unsqueeze(1).to_broadcast([P, ST, D]),
                                       ALU.add).then_inc(s_xb, 1)
                if runs(i, 0):
                    rope(i, u, 0)
                    rope(i, u, 1)
                if runs(i, 4):
                    b = i - 4
                    pool.wait_ge(s_mom, ST * b + ST)
                    apart(pool)
                    pool.tensor_scalar(vareps[:], moments[:, :, 1], 1.0, EPS, ALU.mult, ALU.add).then_inc(s_ve, 1)
                    pool.wait_ge(s_ve, b + 1)
                    pool.tensor_tensor(rstd[:], vareps[:], half_neg[:], ALU.pow).then_inc(s_rstd, 1)

            iterations(pool, body)

            pool.wait_ge(s_route, 3)
            pool.wait_ge(s_x1_out, 16 * B)

            def gather(b, u, first):
                if not first:
                    pool.wait_ge(s_xt, b - 3)
                pool.tensor_copy(id_cur[:, u:u + 1], ids_i[:, bass.ds(b, 1)]).then_inc(s_idc, 1)
                pool.wait_ge(s_idc, b + 1)
                apart(pool)
                pool.indirect_dma_start(out=xg[:, u, :], out_offset=None, in_=x1_dram,
                                        in_offset=bass.IndirectOffsetOnAxis(ap=id_cur[:, u:u + 1], axis=0)
                                        ).then_inc(s_xg[u], 16)

            for b in range(4):
                gather(b, b, True)
            with pool.Fori(0, NBLK // 4 - 1) as trip:
                for u in range(4):
                    gather(4 * trip + (4 + u), u, False)
            for u in range(4):
                pool.wait_ge(s_ys[u], 16 * NBLK // 4)

            def top(t, u, first):
                if not first:
                    pool.wait_ge(s_z, 2 * (t - 4) + 2)
                pool.tensor_copy(slot_cur[:, u, :], slot_i[:, :, bass.ds(t, 1)].rearrange("p k o -> p (k o)")
                                 ).then_inc(s_slc, 1)
                pool.wait_ge(s_slc, t + 1)
                for k in range(TOPK):
                    apart(pool)
                    pool.indirect_dma_start(out=y_top[:, u, k, :], out_offset=None, in_=ys_dram,
                                            in_offset=bass.IndirectOffsetOnAxis(ap=slot_cur[:, u, k:k + 1], axis=0)
                                            ).then_inc(s_yt[u], 16)

            def z_rstd(t, u):
                pool.wait_ge(s_zm, t + 1)
                apart(pool)
                pool.tensor_scalar(z_var[:, u:u + 1], z_moments[:, u, 1:2], 1.0, EPS, ALU.mult, ALU.add).then_inc(s_zv, 1)
                pool.wait_ge(s_zv, t + 1)
                pool.tensor_tensor(z_rs[:, u:u + 1], z_var[:, u:u + 1], half_neg[:, 0:1], ALU.pow).then_inc(s_zr, 1)

            for t in range(4):
                top(t, t, True)
                if t == 3:
                    z_rstd(0, 0)
            with pool.Fori(0, TILES // 4 - 1) as trip:
                for u in range(4):
                    t = 4 * trip + (4 + u)
                    top(t, u, False)
                    z_rstd(t - 3, (u + 1) % 4)
            for t in range(TILES - 3, TILES):
                z_rstd(t, t % 4)

        @block.scalar
        def _(act):
            def empty(i, name, dst, src):
                is_filled(act, i, name)
                nc.scalar.copy(dst, src).then_inc(emptied[name], 1)

            def exp(b, pair, first):
                slot = pair % 4
                act.wait_ge(s_score, 8 * b + pair + 1)
                if pair >= 4:
                    act.wait_ge(filled[f"pv{(pair - 4) // 2}"], b + 1)
                elif not first:
                    act.wait_ge(filled[f"pv{(pair + 4) // 2}"], b)
                nc.scalar.activation(probs[:, slot], ps_score[:, pair % 2], ACT.Exp, scale=SCALE).then_inc(s_exp, 1)

            def body(i, u):
                for step in range(8):
                    lag, pair = (3, step + 2) if step < 6 else (2, step - 6)
                    if runs(i, lag):
                        exp(i - lag, pair, isinstance(i, int) and i == lag)
                    for s, name, ulag in UNITS:
                        if s != step or not runs(i, ulag):
                            continue
                        if name[:2] == "pv":
                            g = int(name[2])
                            if not isinstance(i, int) or i >= 5:
                                act.wait_ge(filled["tr1"], i - 4)
                            empty(i, name, outT[:, 1 - u, g, :], unit(name)[:, 0:S])
                        elif name[:2] == "mt":
                            g = int(name[2])
                            empty(i, name, mT[:, g, :], unit(name, BF16)[0:8, 0:S])
                        elif name[:2] == "tp":
                            l = int(name[2])
                            if not isinstance(i, int) or i >= 2:
                                act.wait_ge(s_planes_out, 16 * (i - 1))
                            empty(i, name, planesT[:, :, l, :], unit(name, BF16).rearrange("p (c t) -> p c t", c=4))
                        elif name == "at":
                            empty(i, name, attnT[:], unit(name).rearrange("p (c t) -> p c t", c=KC))
                        elif name == "xt":
                            empty(i, name, x1T[:], unit(name).rearrange("p (c t) -> p c t", c=KC))

            iterations(act, body)

            act.wait_ge(emptied["lg"], B)
            nc.scalar.activation(r_p, logits[:], ACT.Exp, scale=-1.0).then_inc(s_rexp, 1)

            def xT_out(b, u):
                act.wait_ge(s_xt, b + 1)
                if not isinstance(b, int) or b >= 2:
                    act.wait_ge(s_gu, b - 1)
                nc.scalar.copy(xgT[:, u].rearrange("p c t -> p (c t)"), ps_score[:, 1, 2 * u, :]).then_inc(s_xte, 1)

            def gate_exp(b, u):
                act.wait_ge(s_gu, b + 1)
                if not isinstance(b, int) or b >= 2:
                    act.wait_ge(s_den, b - 1)
                nc.scalar.activation(expg[:, u, :], ps_score[:, 0, 2 * u, 0:I], ACT.Exp, scale=-1.0).then_inc(s_ge, 1)

            def y_out(b, u, u4):
                act.wait_ge(s_y, b + 1)
                if not isinstance(b, int) or b >= 4:
                    act.wait_ge(s_ys[u4], 4 * (b - u4))
                nc.scalar.copy(yb[:, u4, :], ps_unit[:, u, 0:D]).then_inc(s_ye, 1)

            def blk(k, u4):
                full = not isinstance(k, int)
                if full or k < NBLK:
                    xT_out(k, u4 % 2)
                if full or 0 <= k - 1 < NBLK:
                    gate_exp(k - 1, (u4 - 1) % 2)
                if full or 0 <= k - 4 < NBLK:
                    y_out(k - 4, u4 % 2, u4)

            for k in range(8):
                blk(k, k % 4)
            with act.Fori(0, NBLK // 4 - 2) as trip:
                for u4 in range(4):
                    blk(4 * trip + (8 + u4), u4)
            for k in range(NBLK, NBLK + 4):
                blk(k, k % 4)

        @block.vector
        def _(dve):
            V_ = nc.vector
            V_.memset(ones16[:], 1.0).then_inc(s_setup, 1)
            pair = float(np.array([0x3F803F80], np.uint32).view(np.float32)[0])
            k_rows = stacks[QROWS:P, :, 1].rearrange("p a c h t -> p a (c h t)").bitcast(F32)
            V_.memset(k_rows, pair).then_inc(s_setup, 1)
            dve.wait_ge(s_const, 16)
            V_.tensor_copy(ident16[:], c("ident")).then_inc(s_setup, 1)
            V_.tensor_copy(before16[:], c("before")).then_inc(s_setup, 1)
            V_.tensor_copy(iota16[:], c("iota")).then_inc(s_setup, 1)
            V_.tensor_copy(blocks16[:], c("blocks")).then_inc(s_setup, 1)
            dve.wait_ge(s_wqk, 32)
            dve.wait_ge(s_w, 16 * N_W_DMA)
            dve.wait_ge(s_setup_pool, 3)

            def reduce_head(b, h):
                dve.wait_ge(s_max, 16 * b + h + 1)
                V_.tensor_reduce(negmax[:, :, h], ps_max[:, h % 2], X, ALU.max, negate=True).then_inc(s_red, 1)

            def max_planes(b, g):
                dve.wait_ge(s_red, 16 * b + 4 * g + 4)
                m = negmax[:, :, 4 * g:4 * g + 4]
                V_.tensor_copy(mplanes[:, g, :, 0, :], m).then_inc(s_mhi, 1)
                dve.wait_ge(s_mhi, 4 * b + g + 1)
                V_.tensor_tensor(mplanes[:, g, :, 1, :], m, mplanes[:, g, :, 0, :], ALU.subtract).then_inc(s_mpl, 1)

            def unit_out(i, u, name):
                b = i - LAG[name]
                is_filled(dve, i, name)
                if name[:2] == "qk":
                    t = int(name[2])
                    if not isinstance(i, int) or i >= 1:
                        dve.wait_ge(s_rope, 16 * (b - 1) + 8 * t + 3)
                    V_.tensor_tensor(qk[:, t], unit(name), bqk_sb[:], ALU.add).then_inc(emptied[name], 1)
                elif name == "vv":
                    V_.tensor_tensor(V[:, u, :, :, 0:DH], unit(name).rearrange("p (t h d) -> p t h d", t=ST, h=H),
                                     bv_sb[:].rearrange("p (h d) -> p h d", h=H).unsqueeze(1).to_broadcast([P, ST, H, DH]),
                                     ALU.add).then_inc(emptied[name], 1)
                elif name[:2] == "tr":
                    t = int(name[2])
                    r = unit(name).rearrange("p (h j) -> p h j", j=32)
                    V_.reciprocal(inv[:, t, :], r[:, :, DH:DH + 1].rearrange("p h j -> p (h j)")).then_inc(s_inv, 1)
                    dve.wait_ge(s_inv, ST * b + t + 1)
                    V_.tensor_tensor(attn[:, t].rearrange("p (h d) -> p h d", h=H), r[:, :, 0:DH],
                                     inv[:, t, :].unsqueeze(2).to_broadcast([P, H, DH]), ALU.mult).then_inc(emptied[name], 1)
                elif name == "op":
                    dve.wait_ge(s_xb, b + 1)
                    V_.tensor_tensor(y[:], unit(name).rearrange("p (t d) -> p t d", t=ST), xb[:],
                                     ALU.add).then_inc(emptied[name], 1)
                    was_emptied(dve, i, "op")
                    for t in range(ST):
                        V_.bn_stats(stats[:, t, :], y[:, t, :]).then_inc(s_stats, 1)
                    for t in range(ST):
                        dve.wait_ge(s_stats, ST * b + t + 1)
                        apart(dve)
                        V_.bn_aggr(moments[:, t, :], stats[:, t, :]).then_inc(s_mom, 1)
                elif name == "lg":
                    V_.tensor_copy(logits[:, bass.ds(b * ST, ST), :],
                                   unit(name)[:, 0:ST * E].rearrange("p (t e) -> p t e", t=ST)).then_inc(emptied[name], 1)

            def normalise(b, u, first):
                dve.wait_ge(s_rstd, b + 1)
                if not first:
                    dve.wait_ge(s_x1_out, 16 * (b - 1))
                    dve.wait_ge(filled["xt"], b - 1)
                for t in range(ST):
                    V_.tensor_scalar(x1[:, u, t, :], y[:, t, :], moments[:, t, 0:1], rstd[:, t:t + 1],
                                     ALU.subtract, ALU.mult).then_inc(s_x1, 1)

            def body(i, u):
                for step in range(8):
                    if runs(i, 2):
                        reduce_head(i - 2, 2 * step)
                        reduce_head(i - 2, 2 * step + 1)
                        if step % 2:
                            max_planes(i - 2, step // 2)
                    if step == 7 and runs(i, 4):
                        normalise(i - 4, u, isinstance(i, int) and i < 6)
                    for s, name, lag in UNITS:
                        if s == step and name[:2] in ("qk", "vv", "tr", "op", "lg") and runs(i, lag):
                            unit_out(i, u, name)

            iterations(dve, body)

            step = [0]

            def done(ins):
                step[0] += 1
                ins.then_inc(s_r, 1)
                dve.wait_ge(s_r, step[0])

            def row(n):
                return col[:, n, :]

            def over_e(a):
                return a.unsqueeze(2).to_broadcast([P, TILES, E])

            rev = c("rev").unsqueeze(1).to_broadcast([P, TILES, E])
            dve.wait_ge(s_rexp, 1)
            done(V_.tensor_scalar(r_a, r_p, 1.0, None, ALU.add))
            done(V_.reciprocal(r_b, r_a))
            done(V_.reduce_sum(row(0), r_b, X))
            done(V_.reciprocal(row(1), row(0)))
            done(V_.tensor_tensor(r_p, r_b, over_e(row(1)), ALU.mult))
            for k in range(TOPK):
                done(V_.tensor_reduce(row(2 + k), r_p, X, ALU.max))
                done(V_.tensor_tensor(r_a, r_p, over_e(row(2 + k)), ALU.is_equal))
                done(V_.tensor_tensor(r_b, r_a, rev, ALU.mult))
                done(V_.tensor_reduce(row(4), r_b, X, ALU.max))
                done(V_.tensor_tensor(r_oh[k], rev, over_e(row(4)), ALU.is_equal))
                if k == 0:
                    done(V_.scalar_tensor_tensor(out=r_p, in0=r_oh[0], scalar=-4.0, in1=r_p, op0=ALU.mult, op1=ALU.add))
            V_.tensor_tensor(chosen16[:], r_oh[0], r_oh[1], ALU.add).then_inc(s_route, 1)
            done(V_.tensor_tensor(row(5), row(2), row(3), ALU.add))
            done(V_.reciprocal(row(6), row(5)))
            for k in range(TOPK):
                done(V_.tensor_tensor(w_top[:, k, :], row(2 + k), row(6), ALU.mult))
            dve.wait_ge(s_pos, 2)
            cmp = r_big[:, 0:E * TILES].rearrange("p (e j) -> p e j", e=E)
            done(V_.tensor_copy(counts[:, 3, :], ps_max[:, 1, 0, 0:E]))
            done(V_.tensor_tensor(cmp, counts[:, 3, :].unsqueeze(2).to_broadcast([P, E, TILES]),
                                  c("full").unsqueeze(1).to_broadcast([P, E, TILES]), ALU.is_gt))
            done(V_.reduce_sum(counts[:, 0, :], cmp, X))
            low = r_big[:, 0:E * E].rearrange("p (e f) -> p e f", e=E)
            done(V_.tensor_tensor(low, counts[:, 0, :].unsqueeze(1).to_broadcast([P, E, E]),
                                  c("lower").rearrange("p (e f) -> p e f", e=E), ALU.mult))
            done(V_.reduce_sum(counts[:, 1, :], low, X))
            done(V_.tensor_tensor(counts[:, 2, :], counts[:, 0, :], counts[:, 1, :], ALU.add))
            done(V_.scalar_tensor_tensor(out=r_a, in0=counts[:, 1, :].unsqueeze(1).to_broadcast([P, TILES, E]),
                                         scalar=float(P), in1=ps_max[:, 0].rearrange("p t s -> p (t s)").rearrange("p (t e) -> p t e", e=E),
                                         op0=ALU.mult, op1=ALU.add))
            for k in range(TOPK):
                done(V_.tensor_tensor(r_b, r_a, r_oh[k], ALU.mult))
                done(V_.reduce_sum(slot_f[:, k, :], r_b, X))
            done(V_.tensor_copy(slot_i[:], slot_f[:]))
            done(V_.tensor_scalar(part_i[:, 0], slot_i[:], 7, None, ALU.arith_shift_right))
            done(V_.tensor_scalar(part_i[:, 1], slot_i[:], P - 1, None, ALU.bitwise_and))
            done(V_.tensor_copy(part_f[:], part_i[:]))
            ends = r_big[0:1, 0:NBLK * E].rearrange("p (b e) -> p b e", e=E)
            done(V_.tensor_tensor(ends, c("blocks")[0:1].unsqueeze(2).to_broadcast([1, NBLK, E]),
                                  counts[0:1, 2, :].unsqueeze(1).to_broadcast([1, NBLK, E]), ALU.is_ge))
            done(V_.reduce_sum(be_f[:], ends, X))
            V_.tensor_scalar(be_i[:], be_f[:], float(E - 1), None, ALU.min).then_inc(s_route, 1)
            n = 0
            for t in range(TILES):
                for k in range(TOPK):
                    if n >= 4:
                        dve.wait_ge(s_ohu, n - 3)
                    V_.tensor_scalar(oh_in[:, n % 4], iota16[:], part_f[:, 1, k, t:t + 1], None,
                                     ALU.is_equal).then_inc(s_oh, 1)
                    V_.tensor_scalar(oh_blk[:, n % 4], blocks16[:], part_f[:, 0, k, t:t + 1],
                                     c("token")[:, t:t + 1], ALU.is_equal, ALU.mult).then_inc(s_oh, 1)
                    n += 1
            dve.wait_ge(s_ohu, TILES * TOPK)
            done(V_.tensor_scalar(ids_f[:], ps_unit[:, 0, 0:NBLK], float(ID0), None, ALU.add))
            V_.tensor_copy(ids_i[:], ids_f[:]).then_inc(s_route, 1)

            def silu(b, u):
                gate, up = ps_score[:, 0, 2 * u, 0:I], ps_score[:, 0, 2 * u, I:2 * I]
                dve.wait_ge(s_ge, b + 1)
                V_.tensor_scalar(den[:], expg[:, u, :], 1.0, None, ALU.add).then_inc(s_den, 1)
                dve.wait_ge(s_den, b + 1)
                V_.reciprocal(rec[:], den[:]).then_inc(s_rec, 1)
                dve.wait_ge(s_rec, b + 1)
                V_.tensor_tensor(sg[:], gate, rec[:], ALU.mult).then_inc(s_sg, 1)
                dve.wait_ge(s_sg, b + 1)
                if not isinstance(b, int) or b >= 2:
                    dve.wait_ge(s_it, b - 1)
                V_.tensor_tensor(inter[:, u, :], up, sg[:], ALU.mult).then_inc(s_in, 1)

            def interT_out(b, u):
                dve.wait_ge(s_it, b + 1)
                if not isinstance(b, int) or b >= 2:
                    dve.wait_ge(s_y, b - 1)
                V_.tensor_copy(interT[:, u, :], ps_max[:, u, 0, 0:P]).then_inc(s_ite, 1)

            def blk(k, u4):
                full = not isinstance(k, int)
                if full or 0 <= k - 3 < NBLK:
                    interT_out(k - 3, (u4 - 3) % 2)
                if full or 0 <= k - 1 < NBLK:
                    silu(k - 1, (u4 - 1) % 2)

            for k in range(8):
                blk(k, k % 4)
            with dve.Fori(0, NBLK // 4 - 2) as trip:
                for u4 in range(4):
                    blk(4 * trip + (8 + u4), u4)
            for k in range(NBLK, NBLK + 4):
                blk(k, k % 4)

            def combine(t, u):
                dve.wait_ge(s_x1b[u], 4 * (t - u) + 16)
                dve.wait_ge(s_yt[u], 8 * (t - u) + 32)
                V_.scalar_tensor_tensor(out=z[:, u, :], in0=y_top[:, u, 0, :], scalar=w_top[:, 0, bass.ds(t, 1)],
                                        in1=x1b[:, u, :], op0=ALU.mult, op1=ALU.add).then_inc(s_z, 1)
                dve.wait_ge(s_z, 2 * t + 1)
                V_.scalar_tensor_tensor(out=z[:, u, :], in0=y_top[:, u, 1, :], scalar=w_top[:, 1, bass.ds(t, 1)],
                                        in1=z[:, u, :], op0=ALU.mult, op1=ALU.add).then_inc(s_z, 1)
                dve.wait_ge(s_z, 2 * t + 2)
                V_.bn_stats(z_stats[:, u, :], z[:, u, :]).then_inc(s_zs, 1)
                dve.wait_ge(s_zs, t + 1)
                apart(dve)
                V_.bn_aggr(z_moments[:, u, :], z_stats[:, u, :]).then_inc(s_zm, 1)

            def final(t, u, first):
                dve.wait_ge(s_zr, t + 1)
                if not first:
                    dve.wait_ge(s_out[u], 4 * (t - u))
                V_.tensor_scalar(o[:, u, :], z[:, u, :], z_moments[:, u, 0:1], z_rs[:, u:u + 1],
                                 ALU.subtract, ALU.mult).then_inc(s_o, 1)

            for t in range(8):
                combine(t, t % 4)
                if t >= 3:
                    final(t - 3, (t - 3) % 4, t < 7)
            with dve.Fori(0, TILES // 4 - 2) as trip:
                for u in range(4):
                    t = 4 * trip + (8 + u)
                    combine(t, u)
                    final(t - 3, (u + 1) % 4, False)
            for t in range(TILES - 3, TILES):
                final(t, t % 4, False)

        @block.tensor
        def _(pe):
            T = nc.tensor
            ident = c("ident")

            def scores(b, pair, par, first):
                if pair % 2 == 0:
                    pe.wait_ge(s_mrows[pair // 2], 16 * b + 16)
                if not first:
                    pe.wait_ge(s_exp, 8 * b + pair - 1)
                for n in range(2):
                    head = 2 * pair + n
                    for kt in range(ST):
                        mm = T.matmul(ps_score[:, pair % 2, 2 * n + kt, :],
                                      stacks[0:SROWS, par, 1, head // 8, head % 8, kt * P:(kt + 1) * P],
                                      stacks[0:SROWS, par, 0, head // 8, head % 8, :], start=True, stop=True)
                mm.then_inc(s_score, 1)

            def max_scores(b, head, par, first):
                if head % 8 == 0:
                    pe.wait_ge(s_stack[head // 8], 16 * STACK_DMAS * (b + 1))
                if not first:
                    pe.wait_ge(s_red, 16 * b + head - 1)
                for qt in range(ST):
                    mm = T.matmul(ps_max[:, head % 2, qt, :],
                                  stacks[0:QROWS, par, 0, head // 8, head % 8, qt * P:(qt + 1) * P],
                                  stacks[0:QROWS, par, 1, head // 8, head % 8, :], start=True, stop=True)
                mm.then_inc(s_max, 1)

            def fill(i, u, name):
                b, par = i - LAG[name], (u + LAG[name]) % 2
                wait_bank(pe, i, name)
                if name[:2] == "qk":
                    t = int(name[2])
                    pe.wait_ge(s_xqk[par], 8 * (b - par) + 16)
                    for k in range(KC):
                        mm = T.matmul(unit(name), xT_qk[:, par, k, t * P:(t + 1) * P], wqk[:, k, :],
                                      start=(k == 0), stop=(k == KC - 1))
                elif name == "vv":
                    pe.wait_ge(s_xv[par], 8 * (b - par) + 16)
                    for t in range(ST):
                        for k in range(KC):
                            mm = T.matmul(unit(name)[:, t * D:(t + 1) * D], xT_v[:, par, k, t * P:(t + 1) * P],
                                          wv[:, k, :], start=(k == 0), stop=(k == KC - 1))
                elif name[:2] == "tp":
                    l = int(name[2])
                    out4 = unit(name, BF16).rearrange("p (c t) -> p c t", c=4)
                    pe.wait_ge(s_rope, 16 * b + 16)
                    for t in range(ST):
                        for q in range(4):
                            mm = T.transpose(out4[:, q, t * P:(t + 1) * P], planes[:, par, t, l, q * P:(q + 1) * P],
                                             ident16[:])
                elif name[:2] == "mt":
                    g = int(name[2])
                    pe.wait_ge(s_mpl, 4 * b + g + 1)
                    for qt in range(ST):
                        mm = T.transpose(unit(name, BF16)[0:8, qt * P:(qt + 1) * P],
                                         mplanes[:, g, qt].rearrange("p l h -> p (l h)"), ident16[:])
                elif name[:2] == "pv":
                    g = int(name[2])
                    pe.wait_ge(s_exp, 8 * b + 2 * g + 2)
                    was_emptied(pe, b + LAG["vv"], "vv")
                    for kt in range(ST):
                        for n in range(4):
                            pair = 2 * g + n // 2
                            mm = T.matmul(unit(name)[32 * n:32 * n + 32, 0:S], V[:, par, kt, 4 * g + n, :],
                                          probs[:, pair % 4, 2 * (n % 2) + kt, :], start=(kt == 0), stop=(kt == ST - 1))
                elif name[:2] == "tr":
                    t = int(name[2])
                    was_emptied(pe, b + LAG["pv3"], "pv3")
                    for g in range(4):
                        mm = T.transpose(unit(name)[:, g * P:(g + 1) * P], outT[:, par, g, t * P:(t + 1) * P], ident)
                elif name in ("at", "xt"):
                    src = attn if name == "at" else x1[:, par]
                    if name == "at":
                        was_emptied(pe, b + LAG["tr1"], "tr1")
                    else:
                        pe.wait_ge(s_x1, ST * b + ST)
                    for k in range(KC):
                        for t in range(ST):
                            mm = T.transpose(unit(name)[:, k * S + t * P:k * S + (t + 1) * P],
                                             src[:, t, k * P:(k + 1) * P], ident)
                elif name in ("op", "lg"):
                    before, lhs, w, n = ("at", attnT, wo, D) if name == "op" else ("xt", x1T, gw, E)
                    was_emptied(pe, b + LAG[before], before)
                    for t in range(ST):
                        for k in range(KC):
                            mm = T.matmul(unit(name)[:, t * n:(t + 1) * n], lhs[:, k, t * P:(t + 1) * P], w[:, k, :],
                                          start=(k == 0), stop=(k == KC - 1))
                mm.then_inc(filled[name], 1)

            def body(i, u):
                if isinstance(i, int) and i == 1:
                    pe.wait_ge(s_w, 16 * N_W_DMA)
                    pe.wait_ge(s_const, 16)
                    pe.wait_ge(s_setup, 6)
                    pe.wait_ge(s_setup_pool, 3)
                for step in range(8):
                    units = [name for s, name, lag in UNITS if s == step and runs(i, lag)]
                    lag, pair = (3, step + 2) if step < 6 else (2, step - 6)
                    if runs(i, lag):
                        scores(i - lag, pair, (u + lag) % 2, isinstance(i, int) and i == lag == 2)
                    for n in range(max(2, len(units))):
                        if n < 2 and runs(i, 2):
                            max_scores(i - 2, 2 * step + n, u, isinstance(i, int) and i == 2 and step == 0)
                        if n < len(units):
                            fill(i, u, units[n])

            pe.wait_ge(s_wqk, 32)
            iterations(pe, body)

            pe.wait_ge(s_route, 1)
            pos = ps_max[:, 0].rearrange("p t s -> p (t s)")
            T.matmul(pos, before16[:], chosen16[:].rearrange("p t e -> p (t e)"), start=True, stop=False)
            for t in range(TILES - 1):
                after = TILES - 1 - t
                mm = T.matmul(pos[:, (t + 1) * E:].rearrange("p (t e) -> p t e", e=E), ones16[:],
                              chosen16[:, t:t + 1, :].to_broadcast([P, after, E]), start=False, stop=(after == 1))
            mm.then_inc(s_pos, 1)
            for t in range(TILES):
                mm = T.matmul(ps_max[:, 1, 0, 0:E], ones16[:], chosen16[:, t, :], start=(t == 0), stop=(t == TILES - 1))
            mm.then_inc(s_pos, 1)
            for n in range(TILES * TOPK):
                pe.wait_ge(s_oh, 2 * n + 2)
                T.matmul(ps_unit[:, 0, 0:NBLK], oh_in[:, n % 4], oh_blk[:, n % 4], start=(n == 0),
                         stop=(n == TILES * TOPK - 1)).then_inc(s_ohu, 1)

            pe.wait_ge(s_experts, 16 * (KC + 1))

            def expert(b):
                return pe.value_load(be_i[0:1, bass.ds(b, 1)], min_val=0, max_val=E - 1)

            def blk(k, u4):
                full = not isinstance(k, int)
                if full or k < NBLK:
                    u = u4 % 2
                    pe.wait_ge(s_xg[u4], 4 * (k - u4) + 16)
                    if full or k >= 2:
                        pe.wait_ge(s_xte, k - 1)
                    for n in range(KC):
                        mm = T.transpose(ps_score[:, 1, 2 * u, n * P:(n + 1) * P], xg[:, u4, n * P:(n + 1) * P], ident)
                    mm.then_inc(s_xt, 1)
                if full or 0 <= k - 1 < NBLK:
                    b, u = k - 1, (u4 - 1) % 2
                    e = expert(b)
                    pe.wait_ge(s_xte, b + 1)
                    if full or b >= 2:
                        pe.wait_ge(s_in, b - 1)
                    for n in range(KC):
                        mm = T.matmul(ps_score[:, 0, 2 * u, :], xgT[:, u, n, :],
                                      wgu[:, n, bass.ds(e, 1), :].rearrange("p e f -> p (e f)"),
                                      start=(n == 0), stop=(n == KC - 1))
                    mm.then_inc(s_gu, 1)
                if full or 0 <= k - 3 < NBLK:
                    b, u = k - 3, (u4 - 3) % 2
                    pe.wait_ge(s_in, b + 1)
                    if full or b >= 2:
                        pe.wait_ge(s_ite, b - 1)
                    T.transpose(ps_max[:, u, 0, 0:P], inter[:, u, :], ident).then_inc(s_it, 1)
                if full or 0 <= k - 4 < NBLK:
                    b, u = k - 4, u4 % 2
                    e = expert(b)
                    pe.wait_ge(s_ite, b + 1)
                    if full or b >= 2:
                        pe.wait_ge(s_ye, b - 1)
                    T.matmul(ps_unit[:, u, 0:D], interT[:, u, :],
                             wdn[:, bass.ds(e, 1), :].rearrange("p e f -> p (e f)"),
                             start=True, stop=True).then_inc(s_y, 1)

            for k in range(8):
                blk(k, k % 4)
            with pe.Fori(0, NBLK // 4 - 2) as trip:
                for u4 in range(4):
                    blk(4 * trip + (8 + u4), u4)
            for k in range(NBLK, NBLK + 4):
                blk(k, k % 4)


def constants():
    a = np.zeros((P, NCONST), np.float32)

    def put(name, v):
        lo, hi = CONST[name]
        a[:, lo:hi] = np.asarray(v, np.float32).reshape(-1, hi - lo)

    p = np.arange(P)
    put("ident", np.eye(P))
    put("before", p[:, None] < p[None, :])
    inv_freq = (np.float32(1.0) / np.float32(10000.0) ** (np.arange(0, DH, 2, dtype=np.float32) / np.float32(DH)))
    angle = (np.arange(S, dtype=np.float32)[:, None] * inv_freq.astype(np.float32)).astype(np.float32)
    cos, sin = np.cos(angle), np.sin(angle)
    cos = np.concatenate([cos, cos], 1)
    sin = np.concatenate([-sin, sin], 1)
    for name, v in (("cos", cos), ("sin", sin)):
        v = np.repeat(v.reshape(ST, P, DH, 1), 8, axis=3).transpose(1, 0, 2, 3)
        put(name, v.reshape(P, ST * P))
    put("rev", E - np.arange(E))
    put("full", P * np.arange(TILES))
    e = np.arange(E)
    put("lower", e[None, :] < e[:, None])
    put("iota", p)
    put("blocks", np.arange(NBLK))
    put("token", P * np.arange(TILES)[None, :] + p[:, None] - ID0)
    return a


def kernel(L0_attn_x, L0_attn_q_w, L0_attn_k_w, L0_attn_v_w, L0_attn_q_b, L0_attn_k_b, L0_attn_v_b,
           L0_attn_out_w, L0_attn_out_b, L0_ffn_gate_w, L0_ffn_gate_up_proj, L0_ffn_down_proj):
    import concourse.bacc as bacc
    from concourse.bass_utils import run_bass_kernel_spmd

    def arr(v):
        return np.ascontiguousarray(v)

    def by_dim(w):
        w = np.asarray(w)
        return w.reshape(2, 8, DH, -1).transpose(0, 2, 1, 3).reshape(w.shape)

    x = np.asarray(L0_attn_x).reshape(TOK, D)
    bqk = np.concatenate([by_dim(L0_attn_q_b), by_dim(L0_attn_k_b)])
    arrays = {
        "x": arr(x),
        "xT": arr(x.T),
        "wqkT": arr(np.concatenate([by_dim(L0_attn_q_w), by_dim(L0_attn_k_w)]).T),
        "wvT": arr(np.asarray(L0_attn_v_w).T),
        "woT": arr(np.asarray(L0_attn_out_w).T),
        "gateT": arr(np.asarray(L0_ffn_gate_w).T),
        "bqk": arr(np.broadcast_to(bqk, (P, 2 * D))),
        "bv": arr(np.broadcast_to(np.asarray(L0_attn_v_b), (P, D))),
        "bo": arr(np.broadcast_to(np.asarray(L0_attn_out_b), (P, D))),
        "gup": arr(L0_ffn_gate_up_proj),
        "down": arr(L0_ffn_down_proj),
        "const": constants(),
    }
    nc = bacc.Bacc("TRN2", target_bir_lowering=False, num_devices=1)
    args = [nc.dram_tensor(f"in_{name}", a.shape, mybir.dt.from_np(a.dtype), kind="ExternalInput").ap()
            for name, a in arrays.items()]
    out = nc.dram_tensor("out", (TOK, D), F32, kind="ExternalOutput").ap()
    build(nc, *args, out)
    r = run_bass_kernel_spmd(nc, [{f"in_{name}": a for name, a in arrays.items()}], core_ids=[0])
    return r.results[0]["out"].reshape(B, S, D)
```

```python
from contextlib import ExitStack

import concourse.bass as bass
import numpy as np
from concourse import mybir

ALU = mybir.AluOpType
ACT = mybir.ActivationFunctionType
AX = mybir.AxisListType
F32 = mybir.dt.float32
BF16 = mybir.dt.bfloat16
F16 = mybir.dt.float16
I32 = mybir.dt.int32

P = 128
B, S, D = 16, 256, 256
H, DH = 16, 16
E, I, TOPK = 16, 128, 2
TOK = B * S
TILES = TOK // P
KC = D // P
ST = S // P
EPS = 1e-5
SCALE = float(DH) ** -0.5
NBLK = (TOK * TOPK + E * (P - 1)) // P
NBLK += NBLK % 2
ID0 = TOK // 2
GT = 4
GROUPS = TILES // GT
QROWS = 6 * DH
SROWS = QROWS + 2

CONST = {}
_at = 0
for _name, _n in (("ident", P), ("before", P), ("cos", ST * P), ("sin", ST * P), ("rev", E), ("full", TILES),
                  ("lower", E * E), ("iota", P), ("blocks", NBLK), ("token", TILES)):
    CONST[_name] = (_at, _at + _n)
    _at += _n
NCONST = _at

UNITS = [
    (0, "qk0", 0), (0, "pv0", 3), (0, "lg", 5), (0, "mt3", 3),
    (1, "tr0", 4), (1, "tr1", 4),
    (2, "pv1", 3), (2, "at", 4), (2, "mt0", 2),
    (3, "tp0", 1), (3, "op", 4),
    (4, "pv2", 3), (4, "tp1", 1), (4, "qk1", 0),
    (5, "tp2", 1), (5, "vv", 2), (5, "mt1", 2),
    (6, "pv3", 3), (6, "mt2", 2),
    (7, "xt", 4),
]
NAMES = [u[1] for u in UNITS]
LAG = {u[1]: u[2] for u in UNITS}
BANK = {name: n % 2 for n, name in enumerate(NAMES)}
MAXLAG = 5
LOOP_FROM, LOOP_TO, ITERATIONS = 6, B - 2, B + MAXLAG


def runs(i, lag):
    return not isinstance(i, int) or 0 <= i - lag < B


def iterations(engine, body):
    for i in range(LOOP_FROM):
        body(i, i % 2)
    with engine.Fori(0, (LOOP_TO - LOOP_FROM) // 2) as trip:
        for u in range(2):
            body(2 * trip + (LOOP_FROM + u), u)
    for i in range(LOOP_TO, ITERATIONS):
        body(i, i % 2)


def build(nc, x, xT, wqkT, wvT, woT, gateT, bqk, bv, bo, gup, down, const, out):
    x_t = x.rearrange("(t p) d -> p t d", p=P)
    out_t = out.rearrange("(t p) d -> p t d", p=P)
    xT_c = xT.rearrange("(c p) t -> p c t", p=P)

    x1_dram = nc.dram_tensor("x1_dram", (TOK, D), F32).ap()
    ys_dram = nc.dram_tensor("ys_dram", (NBLK * P, D), F32).ap()
    x1_t = x1_dram.rearrange("(t p) d -> p t d", p=P)
    ys_t = ys_dram.rearrange("(b p) d -> p b d", p=P)

    with ExitStack() as ctx:
        def sb(name, shape, dt=F32):
            return ctx.enter_context(nc.sbuf_tensor(name, shape, dt))

        def sem(name):
            return ctx.enter_context(nc.semaphore(name))

        cst = sb("cst", [P, NCONST])
        def c(name):
            a, b = CONST[name]
            return cst[:, a:b]
        ident16 = sb("ident16", [P, P], BF16)
        before16 = sb("before16", [P, P], BF16)
        ones16 = sb("ones16", [P, P], BF16)
        iota16 = sb("iota16", [P, P], F16)
        blocks16 = sb("blocks16", [P, NBLK], F16)
        half_neg = sb("half_neg", [P, GT])
        wqk = sb("wqk", [P, KC, 2 * D])
        wv = sb("wv", [P, KC, D])
        wo = sb("wo", [P, KC, D])
        gw = sb("gw", [P, KC, E])
        bqk_sb = sb("bqk_sb", [P, 2 * D])
        bv_sb = sb("bv_sb", [P, D])
        bo_sb = sb("bo_sb", [P, D])

        xT_qk = sb("xT_qk", [P, 2, KC, S])
        xT_v = sb("xT_v", [P, 2, KC, S])
        xn = sb("xn", [P, 2, ST, D])
        xb = sb("xb", [P, ST, D])
        qk = sb("qk", [P, ST, 2 * D])
        rope_a = sb("rope_a", [P, 2 * D])
        rope_b = sb("rope_b", [P, 2 * D])
        planes = sb("planes", [P, 2, ST, 3, 2 * D], BF16)
        planesT = sb("planesT", [P, 4, 3, S], BF16)
        stacks = sb("stacks", [P, 2, 2, 2, 8, S], BF16)
        V = sb("V", [P, 2, ST, H, 32])
        negmax = sb("negmax", [P, ST, H])
        mplanes = sb("mplanes", [P, 4, ST, 2, 4], BF16)
        mT = sb("mT", [8, 4, S], BF16)
        probs = sb("probs", [P, 4, 4, S])
        outT = sb("outT", [P, 2, 4, S])
        inv = sb("inv", [P, ST, H])
        attn = sb("attn", [P, ST, D])
        attnT = sb("attnT", [P, KC, S])
        y = sb("y", [P, ST, D])
        stats = sb("stats", [P, ST, 6])
        moments = sb("moments", [P, ST, 2])
        vareps = sb("vareps", [P, ST])
        rstd = sb("rstd", [P, ST])
        x1 = sb("x1", [P, 2, ST, D])
        x1T = sb("x1T", [P, KC, S])
        logits = sb("logits", [P, TILES, E])

        wgu = sb("wgu", [P, KC, E, 2 * I])
        late = stacks[:].rearrange("p a b c h t -> p (a b c h t)").bitcast(F32)
        wgu_flat = wgu[:].rearrange("p c e f -> p c (e f)")
        wdn_flat = late[:, 0:E * D]
        wdn = wdn_flat.rearrange("p (e h) -> p e h", e=E)
        y_top = late[:, E * D:2 * E * D].rearrange("p (u a k h) -> p u a k h", u=2, a=GT, k=TOPK)
        probs_f = probs[:].rearrange("p a b s -> p (a b s)")
        R = TILES * E
        r_p = probs_f[:, 0:R].rearrange("p (t e) -> p t e", e=E)
        r_a = probs_f[:, R:2 * R].rearrange("p (t e) -> p t e", e=E)
        r_b = probs_f[:, 2 * R:3 * R].rearrange("p (t e) -> p t e", e=E)
        r_oh = [probs_f[:, (3 + k) * R:(4 + k) * R].rearrange("p (t e) -> p t e", e=E) for k in range(2)]
        r_big = probs_f[:, 5 * R:5 * R + NBLK * E]
        x1b = probs_f[:, 0:2 * GT * D].rearrange("p (u a h) -> p u a h", u=2, a=GT)
        o = probs_f[:, 2 * GT * D:4 * GT * D].rearrange("p (u a h) -> p u a h", u=2, a=GT)
        col = sb("col", [P, 8, TILES])
        w_top = sb("w_top", [P, 2, TILES])
        chosen16 = sb("chosen16", [P, TILES, E], BF16)
        counts = sb("counts", [P, 4, E])
        slot_f = sb("slot_f", [P, 2, TILES])
        slot_i = sb("slot_i", [P, 2, TILES], I32)
        part_i = sb("part_i", [P, 2, 2, TILES], I32)
        part_f = sb("part_f", [P, 2, 2, TILES])
        oh_in = sb("oh_in", [P, 4, P], F16)
        oh_blk = sb("oh_blk", [P, 4, NBLK], F16)
        ids_f = sb("ids_f", [P, NBLK])
        ids_i = sb("ids_i", [P, NBLK], I32)
        be_f = sb("be_f", [1, NBLK])
        be_i = sb("be_i", [1, NBLK], I32)
        id_cur = sb("id_cur", [P, 8], I32)
        xg = planes[:].rearrange("p u t l n -> p (u t l n)").bitcast(F32)[:, 0:8 * D].rearrange("p (a h) -> p a h", a=8)
        xgT = sb("xgT", [P, 2, KC, P])
        sg = sb("sg", [P, 2, I])
        inter = sb("inter", [P, 2, I])
        interT = sb("interT", [P, 2, P])
        yb = sb("yb", [P, 4, D])
        slot_cur = sb("slot_cur", [P, 2, TOPK, GT], I32)
        z = sb("z", [P, 2, GT, D])
        z_stats = sb("z_stats", [P, 2, GT, 6])
        z_moments = sb("z_moments", [P, 2, GT, 2])
        z_var = sb("z_var", [P, 2, GT])
        z_rs = sb("z_rs", [P, 2, GT])

        ps_score = ctx.enter_context(nc.psum_tensor("ps_score", [P, 2, 4, S], F32))
        ps_max = ctx.enter_context(nc.psum_tensor("ps_max", [P, 2, ST, S], F32))
        ps_unit = ctx.enter_context(nc.psum_tensor("ps_unit", [P, 2, 512], F32))

        s_const, s_wqk, s_w, s_experts = (sem("const_loaded"), sem("qk_weights_loaded"), sem("weights_loaded"),
                                          sem("experts_loaded"))
        s_setup, s_setup_pool = sem("setup_vector"), sem("setup_pool")
        s_xqk = [sem(f"xT_qk_loaded{u}") for u in range(2)]
        s_xv = [sem(f"xT_v_loaded{u}") for u in range(2)]
        s_xn = [sem(f"xn_loaded{u}") for u in range(2)]
        s_stack = [sem(f"stack_half_loaded{u}") for u in range(2)]
        s_mrows = [sem(f"max_rows_loaded{g}") for g in range(4)]
        s_x1_out = sem("x1_written")
        filled = {n: sem(f"filled_{n}") for n in NAMES}
        emptied = {n: sem(f"emptied_{n}") for n in NAMES}
        s_score, s_exp = sem("score_pair_filled"), sem("exp_pair_done")
        s_max, s_red = sem("max_head_filled"), sem("max_head_reduced")
        s_mhi, s_mpl = sem("max_high_plane"), sem("max_planes_done")
        s_rope = sem("rope_step")
        s_xb, s_inv = sem("x_with_bias"), sem("sums_inverted")
        s_stats, s_mom, s_ve, s_rstd, s_x1 = (sem("ln_stats"), sem("ln_moments"), sem("ln_var_eps"),
                                             sem("ln_rstd"), sem("x1_done"))
        s_rexp, s_r = sem("router_exp"), sem("router_step")
        s_pos = sem("positions_filled")
        s_oh, s_ohu = sem("one_hots_done"), sem("one_hots_used")
        s_route = sem("routing_done")
        s_idc, s_xg = sem("block_ids_copied"), [sem(f"rows_gathered{u}") for u in range(8)]
        s_xt, s_xte = sem("block_xT_filled"), sem("block_xT_emptied")
        s_gu, s_sg, s_in = sem("gate_up_filled"), sem("gate_silu_done"), sem("inter_done")
        s_it, s_ite = sem("interT_filled"), sem("interT_emptied")
        s_y, s_ye = sem("block_y_filled"), sem("block_y_emptied")
        s_ys = [sem(f"block_y_written{u}") for u in range(4)]
        s_slc, s_yt = sem("slots_copied"), [[sem(f"y_gathered{u}_{n}") for n in range(GT)] for u in range(2)]
        s_x1b = [sem(f"x1_reloaded{u}") for u in range(2)]
        s_z, s_zs, s_zm, s_zv, s_zr, s_o = (sem("z_step"), sem("z_stats"), sem("z_moments"), sem("z_var_eps"),
                                            sem("z_rstd"), sem("out_done"))
        s_out = [sem(f"out_written{u}") for u in range(2)]

        def unit(name, dt=F32):
            bank = ps_unit[:, BANK[name], :]
            return bank if dt == F32 else bank.bitcast(dt)

        def wait_bank(pe, i, name):
            n = NAMES.index(name)
            for back in range(1, len(UNITS) * (MAXLAG + 2)):
                m = n - back
                turn = i + (m // len(UNITS))
                other = NAMES[m % len(UNITS)]
                if BANK[other] == BANK[name] and runs(turn, LAG[other]):
                    if isinstance(turn, int) and turn < 0:
                        return
                    pe.wait_ge(emptied[other], turn - LAG[other] + 1)
                    return

        def is_filled(engine, i, name):
            engine.wait_ge(filled[name], i - LAG[name] + 1)

        def was_emptied(engine, i, name):
            engine.wait_ge(emptied[name], i - LAG[name] + 1)

        def apart(engine):
            engine.nop(nofuse=True)

        N_W_DMA = 5
        STACK_DMAS = 12
        STACK_AT = (0, 3 * DH, 5 * DH)
        X = AX.X

        block = ctx.enter_context(nc.Block())

        @block.sync
        def _(sp):
            sp.dma_start(xT_qk[:, 0], xT_c[:, :, 0:S]).then_inc(s_xqk[0], 16)
            sp.dma_start(wqk[:], wqkT.rearrange("(c p) n -> p c n", p=P)).then_inc(s_wqk, 16)
            sp.dma_start(bqk_sb[:], bqk).then_inc(s_wqk, 16)
            sp.dma_start(cst[:], const).then_inc(s_const, 16)
            for dst, src in ((wv[:], wvT.rearrange("(c p) n -> p c n", p=P)),
                             (wo[:], woT.rearrange("(c p) n -> p c n", p=P)),
                             (gw[:], gateT.rearrange("(c p) n -> p c n", p=P)), (bv_sb[:], bv), (bo_sb[:], bo)):
                sp.dma_start(dst, src).then_inc(s_w, 16)

            def stack_plane(b, u, hh, l):
                for j in range(3 - l):
                    at = STACK_AT[j] + l * DH
                    sp.dma_start(stacks[at:at + DH, u, 0, hh], planesT[:, hh, l, :]).then_inc(s_stack[hh], 16)
                for r in range(3 - l):
                    at = STACK_AT[l] + r * DH
                    sp.dma_start(stacks[at:at + DH, u, 1, hh], planesT[:, 2 + hh, l, :]).then_inc(s_stack[hh], 16)

            def body(i, u):
                if runs(i + 1, 0):
                    if not isinstance(i, int) or i >= 1:
                        sp.wait_ge(filled["qk1"], i)
                    sp.dma_start(xT_qk[:, 1 - u], xT_c[:, :, bass.ds((i + 1) * S, S)]).then_inc(s_xqk[1 - u], 16)
                if runs(i, 1):
                    if not isinstance(i, int) or i >= 3:
                        sp.wait_ge(filled["vv"], i - 2)
                    sp.dma_start(xT_v[:, 1 - u], xT_c[:, :, bass.ds((i - 1) * S, S)]).then_inc(s_xv[1 - u], 16)
                if runs(i, 3):
                    if not isinstance(i, int) or i >= 5:
                        sp.wait_ge(s_xb, i - 4)
                    sp.dma_start(xn[:, 1 - u], x_t[:, bass.ds((i - 3) * ST, ST), :]).then_inc(s_xn[1 - u], 16)
                if runs(i, 1):
                    for l in range(3):
                        was_emptied(sp, i, f"tp{l}")
                        if l == 0 and runs(i, 3):
                            sp.wait_ge(s_score, 8 * (i - 3) + 4)
                        stack_plane(i - 1, 1 - u, 0, l)
                    if runs(i, 3):
                        sp.wait_ge(s_score, 8 * (i - 3) + 8)
                    for l in range(3):
                        stack_plane(i - 1, 1 - u, 1, l)
                if runs(i, 4):
                    sp.wait_ge(s_x1, ST * (i - 4) + ST)
                    sp.dma_start(x1_t[:, bass.ds((i - 4) * ST, ST), :], x1[:, u]).then_inc(s_x1_out, 16)
                if isinstance(i, int) and i == 2:
                    for chunk in range(KC):
                        sp.dma_start(wgu[:, chunk], gup[:, chunk * P:(chunk + 1) * P, :].rearrange("e p f -> p e f")
                                     ).then_inc(s_experts, 16)
                if isinstance(i, int) and i == B + 2:
                    sp.wait_ge(s_score, 8 * B)
                    sp.dma_start(wdn, down.rearrange("e p h -> p e h")).then_inc(s_experts, 16)

            iterations(sp, body)

            with sp.Fori(0, NBLK // 4) as trip:
                for u in range(4):
                    b = 4 * trip + u
                    sp.wait_ge(s_ye, b + 1)
                    sp.dma_start(ys_t[:, bass.ds(b, 1), :], yb[:, u:u + 1, :]).then_inc(s_ys[u], 16)
            def reload(g, u):
                sp.dma_start(x1b[:, u], x1_t[:, bass.ds(GT * g, GT), :]).then_inc(s_x1b[u], 16)

            def store(g, u):
                sp.wait_ge(s_o, GT * g + GT)
                sp.dma_start(out_t[:, bass.ds(GT * g, GT), :], o[:, u]).then_inc(s_out[u], 16)

            sp.wait_ge(s_route, 3)
            for g in range(2):
                reload(g, g)
            with sp.Fori(0, GROUPS // 2 - 1) as trip:
                for u in range(2):
                    g = 2 * trip + u
                    sp.wait_ge(s_z, 2 * GT * g + 2 * GT)
                    reload(g + 2, u)
                    store(g, u)
            store(GROUPS - 2, 0)
            for n in range(0, GT, 2):
                t = TILES - GT + n
                sp.wait_ge(s_o, t + 2)
                sp.dma_start(out_t[:, t:t + 2, :], o[:, 1, n:n + 2]).then_inc(s_out[1], 16)
            sp.wait_ge(s_out[0], 16 * GROUPS // 2)
            sp.wait_ge(s_out[1], 16 * (GROUPS // 2 - 1 + GT // 2))

        @block.gpsimd
        def _(pool):
            pool.memset(half_neg[:], -0.5).then_inc(s_setup_pool, 1)
            pool.memset(V[:], 0.0).then_inc(s_setup_pool, 1)
            pool.wait_ge(s_setup_pool, 2)
            pool.memset(V[:, :, :, :, DH:DH + 1], 1.0).then_inc(s_setup_pool, 1)
            pool.wait_ge(s_const, 16)
            pool.wait_ge(s_w, 16 * N_W_DMA)

            def rope(i, u, t):
                n = 16 * i + 8 * t
                cos = c("cos")[:, t * P:(t + 1) * P].unsqueeze(1).to_broadcast([P, 4, P])
                sin = c("sin")[:, t * P:(t + 1) * P]
                q4 = qk[:, t].rearrange("p (c n) -> p c n", c=4)
                a4 = rope_a[:].rearrange("p (c n) -> p c n", c=4)
                b4 = rope_b[:].rearrange("p (c n) -> p c n", c=4)
                h = P // 2
                if not isinstance(i, int) or n > 0:
                    pool.wait_ge(s_rope, n)
                pool.wait_ge(emptied[f"qk{t}"], i + 1)
                pool.tensor_tensor(a4, q4, cos, ALU.mult).then_inc(s_rope, 1)
                for lo, other in ((0, h), (h, 0)):
                    pool.tensor_tensor(b4[:, :, lo:lo + h], q4[:, :, other:other + h],
                                       sin[:, lo:lo + h].unsqueeze(1).to_broadcast([P, 4, h]),
                                       ALU.mult).then_inc(s_rope, 1)
                pool.wait_ge(s_rope, n + 3)
                pool.tensor_tensor(rope_a[:], rope_a[:], rope_b[:], ALU.add).then_inc(s_rope, 1)
                if not isinstance(i, int) or i >= 2:
                    pool.wait_ge(filled["tp2"], i - 1)
                pool.wait_ge(s_rope, n + 4)
                apart(pool)
                pool.tensor_scalar(planes[:, u, t, 0], rope_a[:], 1.0, 0.0, ALU.mult, ALU.add).then_inc(s_rope, 1)
                pool.wait_ge(s_rope, n + 5)
                pool.tensor_tensor(rope_b[:], rope_a[:], planes[:, u, t, 0], ALU.subtract).then_inc(s_rope, 1)
                pool.wait_ge(s_rope, n + 6)
                apart(pool)
                pool.tensor_scalar(planes[:, u, t, 1], rope_b[:], 1.0, 0.0, ALU.mult, ALU.add).then_inc(s_rope, 1)
                pool.wait_ge(s_rope, n + 7)
                pool.tensor_tensor(planes[:, u, t, 2], rope_b[:], planes[:, u, t, 1], ALU.subtract).then_inc(s_rope, 1)

            def body(i, u):
                if runs(i, 4):
                    b = i - 4
                    pool.wait_ge(s_xn[u], 8 * (b - u) + 16)
                    if not isinstance(i, int) or i >= 5:
                        pool.wait_ge(emptied["op"], b)
                    pool.tensor_tensor(xb[:], xn[:, u], bo_sb[:].unsqueeze(1).to_broadcast([P, ST, D]),
                                       ALU.add).then_inc(s_xb, 1)
                if runs(i, 0):
                    rope(i, u, 0)
                if runs(i, 4):
                    pool.wait_ge(s_mom, ST * b + ST)
                    apart(pool)
                    pool.tensor_scalar(vareps[:], moments[:, :, 1], 1.0, EPS, ALU.mult, ALU.add).then_inc(s_ve, 1)
                    pool.wait_ge(s_ve, b + 1)
                    pool.tensor_tensor(rstd[:], vareps[:], half_neg[:, 0:ST], ALU.pow).then_inc(s_rstd, 1)
                if runs(i, 0):
                    rope(i, u, 1)

            iterations(pool, body)

            pool.wait_ge(s_route, 3)
            pool.wait_ge(s_x1_out, 16 * B)

            def gather(b, u, group, first):
                if u % 4 == 0:
                    pool.wait_ge(s_idc, group + 1)
                if not first:
                    pool.wait_ge(s_xt, b - 7)
                apart(pool)
                pool.indirect_dma_start(out=xg[:, u, :], out_offset=None, in_=x1_dram,
                                        in_offset=bass.IndirectOffsetOnAxis(ap=id_cur[:, u:u + 1], axis=0)
                                        ).then_inc(s_xg[u], 16)

            for u in range(8):
                gather(u, u, u // 4, True)
            with pool.Fori(0, NBLK // 8 - 1) as trip:
                for u in range(8):
                    gather(8 * trip + (8 + u), u, 2 * trip + (2 + u // 4), False)
            for u in range(4):
                pool.wait_ge(s_ys[u], 16 * NBLK // 4)

            def top(g, u, first):
                pool.wait_ge(s_slc, g + 1)
                for n in range(GT):
                    if not first:
                        pool.wait_ge(s_z, 2 * GT * (g - 2) + 4 * (n // 2) + 4)
                    for k in range(TOPK):
                        apart(pool)
                        pool.indirect_dma_start(out=y_top[:, u, n, k, :], out_offset=None, in_=ys_dram,
                                                in_offset=bass.IndirectOffsetOnAxis(ap=slot_cur[:, u, k, n:n + 1], axis=0)
                                                ).then_inc(s_yt[u][n], 16)

            def z_rstd(g, u):
                pool.wait_ge(s_zm, GT * g + GT)
                apart(pool)
                pool.tensor_scalar(z_var[:, u], z_moments[:, u, :, 1], 1.0, EPS, ALU.mult, ALU.add).then_inc(s_zv, 1)
                pool.wait_ge(s_zv, g + 1)
                pool.tensor_tensor(z_rs[:, u], z_var[:, u], half_neg[:], ALU.pow).then_inc(s_zr, 1)

            top(0, 0, True)
            top(1, 1, True)
            z_rstd(0, 0)
            with pool.Fori(0, GROUPS // 2 - 1) as trip:
                for u in range(2):
                    g = 2 * trip + (2 + u)
                    top(g, u, False)
                    z_rstd(g - 1, 1 - u)
            z_rstd(GROUPS - 1, 1)

        @block.scalar
        def _(act):
            def empty(i, name, dst, src):
                is_filled(act, i, name)
                nc.scalar.copy(dst, src).then_inc(emptied[name], 1)

            def exp(b, pair, first):
                slot = pair % 4
                act.wait_ge(s_score, 8 * b + pair + 1)
                if pair >= 4:
                    act.wait_ge(filled[f"pv{(pair - 4) // 2}"], b + 1)
                elif not first:
                    act.wait_ge(filled[f"pv{(pair + 4) // 2}"], b)
                nc.scalar.activation(probs[:, slot], ps_score[:, pair % 2], ACT.Exp, scale=SCALE).then_inc(s_exp, 1)

            def body(i, u):
                for step in range(8):
                    lag, pair = (3, step + 2) if step < 6 else (2, step - 6)
                    if runs(i, lag):
                        exp(i - lag, pair, isinstance(i, int) and i == lag)
                    for s, name, ulag in UNITS:
                        if s != step or not runs(i, ulag):
                            continue
                        if name[:2] == "pv":
                            g = int(name[2])
                            if not isinstance(i, int) or i >= 5:
                                act.wait_ge(filled["tr1"], i - 4)
                            empty(i, name, outT[:, 1 - u, g, :], unit(name)[:, 0:S])
                        elif name[:2] == "mt":
                            g = int(name[2])
                            empty(i, name, mT[:, g, :], unit(name, BF16)[0:8, 0:S])
                            was_emptied(act, i, name)
                            act.dma_start(stacks[QROWS:SROWS, (u + ulag) % 2, 0, g // 2, 4 * (g % 2):4 * (g % 2) + 4, :],
                                          mT[:, g, :]).then_inc(s_mrows[g], 16)
                        elif name[:2] == "tp":
                            l = int(name[2])
                            if not isinstance(i, int) or i >= 2:
                                for half in s_stack:
                                    act.wait_ge(half, 16 * STACK_DMAS * (i - 1))
                            empty(i, name, planesT[:, :, l, :], unit(name, BF16).rearrange("p (c t) -> p c t", c=4))
                        elif name == "at":
                            empty(i, name, attnT[:], unit(name).rearrange("p (c t) -> p c t", c=KC))
                        elif name == "xt":
                            empty(i, name, x1T[:], unit(name).rearrange("p (c t) -> p c t", c=KC))

            iterations(act, body)

            act.wait_ge(emptied["lg"], B)
            nc.scalar.activation(r_p, logits[:], ACT.Exp, scale=-1.0).then_inc(s_rexp, 1)

            act.wait_ge(s_route, 3)

            def ids_copy(g, h):
                nc.scalar.copy(id_cur[:, 4 * h:4 * h + 4], ids_i[:, bass.ds(4 * g, 4)]).then_inc(s_idc, 1)

            def xT_out(b, u):
                act.wait_ge(s_xt, b + 1)
                if not isinstance(b, int) or b >= 2:
                    act.wait_ge(s_gu, b - 1)
                nc.scalar.copy(xgT[:, u].rearrange("p c t -> p (c t)"), ps_score[:, 0, 2 * u, :]).then_inc(s_xte, 1)

            def silu(b, u):
                act.wait_ge(s_gu, b + 1)
                if not isinstance(b, int) or b >= 2:
                    act.wait_ge(s_in, b - 1)
                nc.scalar.activation(sg[:, u, :], ps_score[:, 1, 2 * u, 0:P], ACT.Silu).then_inc(s_sg, 1)

            def blk(k, u8, trip8):
                full = not isinstance(k, int)
                if u8 % 4 == 0 and (full or k + 4 < NBLK) and (full or k > 0):
                    ids_copy(2 * trip8 + (u8 // 4 + 1), (u8 // 4 + 1) % 2)
                if full or k < NBLK:
                    xT_out(k, u8 % 2)
                if full or 0 <= k - 1 < NBLK:
                    silu(k - 1, (u8 - 1) % 2)

            ids_copy(0, 0)
            ids_copy(1, 1)
            for k in range(8):
                blk(k, k, 0)
            with act.Fori(0, NBLK // 8 - 2) as trip:
                for u8 in range(8):
                    blk(8 * trip + (8 + u8), u8, trip + 1)
            for k in range(NBLK - 8, NBLK + 1):
                blk(k, k % 8, k // 8)

            def slots_copy(g, u, first):
                if not first:
                    act.wait_ge(s_z, 2 * GT * (g - 1))
                nc.scalar.copy(slot_cur[:, u], slot_i[:, :, bass.ds(GT * g, GT)]).then_inc(s_slc, 1)

            slots_copy(0, 0, True)
            slots_copy(1, 1, True)
            with act.Fori(0, GROUPS // 2 - 1) as trip:
                for u in range(2):
                    slots_copy(2 * trip + (2 + u), u, False)

        @block.vector
        def _(dve):
            V_ = nc.vector
            V_.memset(ones16[:], 1.0).then_inc(s_setup, 1)
            pair = float(np.array([0x3F803F80], np.uint32).view(np.float32)[0])
            k_rows = stacks[QROWS:P, :, 1].rearrange("p a c h t -> p a (c h t)").bitcast(F32)
            V_.memset(k_rows, pair).then_inc(s_setup, 1)
            dve.wait_ge(s_const, 16)
            V_.tensor_copy(ident16[:], c("ident")).then_inc(s_setup, 1)
            V_.tensor_copy(before16[:], c("before")).then_inc(s_setup, 1)
            V_.tensor_copy(iota16[:], c("iota")).then_inc(s_setup, 1)
            V_.tensor_copy(blocks16[:], c("blocks")).then_inc(s_setup, 1)
            dve.wait_ge(s_wqk, 32)
            dve.wait_ge(s_w, 16 * N_W_DMA)
            dve.wait_ge(s_setup_pool, 3)

            def reduce_head(b, h):
                dve.wait_ge(s_max, 16 * b + h + 1)
                V_.tensor_reduce(negmax[:, :, h], ps_max[:, h % 2], X, ALU.max, negate=True).then_inc(s_red, 1)

            def max_planes(b, g):
                dve.wait_ge(s_red, 16 * b + 4 * g + 4)
                m = negmax[:, :, 4 * g:4 * g + 4]
                V_.tensor_copy(mplanes[:, g, :, 0, :], m).then_inc(s_mhi, 1)
                dve.wait_ge(s_mhi, 4 * b + g + 1)
                V_.tensor_tensor(mplanes[:, g, :, 1, :], m, mplanes[:, g, :, 0, :], ALU.subtract).then_inc(s_mpl, 1)

            def unit_out(i, u, name):
                b = i - LAG[name]
                is_filled(dve, i, name)
                if name[:2] == "qk":
                    t = int(name[2])
                    if not isinstance(i, int) or i >= 1:
                        dve.wait_ge(s_rope, 16 * (b - 1) + 8 * t + 3)
                    V_.tensor_tensor(qk[:, t], unit(name), bqk_sb[:], ALU.add).then_inc(emptied[name], 1)
                elif name == "vv":
                    V_.tensor_tensor(V[:, u, :, :, 0:DH], unit(name).rearrange("p (t h d) -> p t h d", t=ST, h=H),
                                     bv_sb[:].rearrange("p (h d) -> p h d", h=H).unsqueeze(1).to_broadcast([P, ST, H, DH]),
                                     ALU.add).then_inc(emptied[name], 1)
                elif name[:2] == "tr":
                    t = int(name[2])
                    r = unit(name).rearrange("p (h j) -> p h j", j=32)
                    V_.reciprocal(inv[:, t, :], r[:, :, DH:DH + 1].rearrange("p h j -> p (h j)")).then_inc(s_inv, 1)
                    dve.wait_ge(s_inv, ST * b + t + 1)
                    V_.tensor_tensor(attn[:, t].rearrange("p (h d) -> p h d", h=H), r[:, :, 0:DH],
                                     inv[:, t, :].unsqueeze(2).to_broadcast([P, H, DH]), ALU.mult).then_inc(emptied[name], 1)
                elif name == "op":
                    dve.wait_ge(s_xb, b + 1)
                    V_.tensor_tensor(y[:], unit(name).rearrange("p (t d) -> p t d", t=ST), xb[:],
                                     ALU.add).then_inc(emptied[name], 1)
                    was_emptied(dve, i, "op")
                    for t in range(ST):
                        V_.bn_stats(stats[:, t, :], y[:, t, :]).then_inc(s_stats, 1)
                    for t in range(ST):
                        dve.wait_ge(s_stats, ST * b + t + 1)
                        apart(dve)
                        V_.bn_aggr(moments[:, t, :], stats[:, t, :]).then_inc(s_mom, 1)
                elif name == "lg":
                    V_.tensor_copy(logits[:, bass.ds(b * ST, ST), :],
                                   unit(name)[:, 0:ST * E].rearrange("p (t e) -> p t e", t=ST)).then_inc(emptied[name], 1)

            def normalise(b, u, first):
                dve.wait_ge(s_rstd, b + 1)
                if not first:
                    dve.wait_ge(s_x1_out, 16 * (b - 1))
                    dve.wait_ge(filled["xt"], b - 1)
                for t in range(ST):
                    V_.tensor_scalar(x1[:, u, t, :], y[:, t, :], moments[:, t, 0:1], rstd[:, t:t + 1],
                                     ALU.subtract, ALU.mult).then_inc(s_x1, 1)

            def body(i, u):
                for step in range(8):
                    units = [name for s, name, lag in UNITS if s == step and runs(i, lag)]
                    for n in range(max(2, len(units))):
                        if n < 2 and runs(i, 2):
                            reduce_head(i - 2, 2 * step + n)
                            if n == 1 and step % 2:
                                max_planes(i - 2, step // 2)
                        if n < len(units) and units[n][:2] in ("qk", "vv", "tr", "op", "lg"):
                            unit_out(i, u, units[n])
                    if step == 5 and runs(i, 4):
                        normalise(i - 4, u, isinstance(i, int) and i < 6)

            iterations(dve, body)

            step = [0]

            def done(ins):
                step[0] += 1
                ins.then_inc(s_r, 1)
                dve.wait_ge(s_r, step[0])

            def row(n):
                return col[:, n, :]

            def over_e(a):
                return a.unsqueeze(2).to_broadcast([P, TILES, E])

            rev = c("rev").unsqueeze(1).to_broadcast([P, TILES, E])
            dve.wait_ge(s_rexp, 1)
            done(V_.tensor_scalar(r_a, r_p, 1.0, None, ALU.add))
            done(V_.reciprocal(r_b, r_a))
            done(V_.reduce_sum(row(0), r_b, X))
            done(V_.reciprocal(row(1), row(0)))
            done(V_.tensor_tensor(r_p, r_b, over_e(row(1)), ALU.mult))
            for k in range(TOPK):
                done(V_.tensor_reduce(row(2 + k), r_p, X, ALU.max))
                done(V_.tensor_tensor(r_a, r_p, over_e(row(2 + k)), ALU.is_equal))
                done(V_.tensor_tensor(r_b, r_a, rev, ALU.mult))
                done(V_.tensor_reduce(row(4), r_b, X, ALU.max))
                done(V_.tensor_tensor(r_oh[k], rev, over_e(row(4)), ALU.is_equal))
                if k == 0:
                    done(V_.scalar_tensor_tensor(out=r_p, in0=r_oh[0], scalar=-4.0, in1=r_p, op0=ALU.mult, op1=ALU.add))
            V_.tensor_tensor(chosen16[:], r_oh[0], r_oh[1], ALU.add).then_inc(s_route, 1)
            done(V_.tensor_tensor(row(5), row(2), row(3), ALU.add))
            done(V_.reciprocal(row(6), row(5)))
            for k in range(TOPK):
                done(V_.tensor_tensor(w_top[:, k, :], row(2 + k), row(6), ALU.mult))
            dve.wait_ge(s_pos, 2)
            cmp = r_big[:, 0:E * TILES].rearrange("p (e j) -> p e j", e=E)
            done(V_.tensor_copy(counts[:, 3, :], ps_max[:, 1, 0, 0:E]))
            done(V_.tensor_tensor(cmp, counts[:, 3, :].unsqueeze(2).to_broadcast([P, E, TILES]),
                                  c("full").unsqueeze(1).to_broadcast([P, E, TILES]), ALU.is_gt))
            done(V_.reduce_sum(counts[:, 0, :], cmp, X))
            low = r_big[:, 0:E * E].rearrange("p (e f) -> p e f", e=E)
            done(V_.tensor_tensor(low, counts[:, 0, :].unsqueeze(1).to_broadcast([P, E, E]),
                                  c("lower").rearrange("p (e f) -> p e f", e=E), ALU.mult))
            done(V_.reduce_sum(counts[:, 1, :], low, X))
            done(V_.tensor_tensor(counts[:, 2, :], counts[:, 0, :], counts[:, 1, :], ALU.add))
            done(V_.scalar_tensor_tensor(out=r_a, in0=counts[:, 1, :].unsqueeze(1).to_broadcast([P, TILES, E]),
                                         scalar=float(P), in1=ps_max[:, 0].rearrange("p t s -> p (t s)").rearrange("p (t e) -> p t e", e=E),
                                         op0=ALU.mult, op1=ALU.add))
            for k in range(TOPK):
                done(V_.tensor_tensor(r_b, r_a, r_oh[k], ALU.mult))
                done(V_.reduce_sum(slot_f[:, k, :], r_b, X))
            done(V_.tensor_copy(slot_i[:], slot_f[:]))
            done(V_.tensor_scalar(part_i[:, 0], slot_i[:], 7, None, ALU.arith_shift_right))
            done(V_.tensor_scalar(part_i[:, 1], slot_i[:], P - 1, None, ALU.bitwise_and))
            done(V_.tensor_copy(part_f[:], part_i[:]))
            ends = r_big[0:1, 0:NBLK * E].rearrange("p (b e) -> p b e", e=E)
            done(V_.tensor_tensor(ends, c("blocks")[0:1].unsqueeze(2).to_broadcast([1, NBLK, E]),
                                  counts[0:1, 2, :].unsqueeze(1).to_broadcast([1, NBLK, E]), ALU.is_ge))
            done(V_.reduce_sum(be_f[:], ends, X))
            V_.tensor_scalar(be_i[:], be_f[:], float(E - 1), float(D), ALU.min, ALU.mult).then_inc(s_route, 1)
            n = 0
            for t in range(TILES):
                for k in range(TOPK):
                    if n >= 4:
                        dve.wait_ge(s_ohu, n - 3)
                    V_.tensor_scalar(oh_in[:, n % 4], iota16[:], part_f[:, 1, k, t:t + 1], None,
                                     ALU.is_equal).then_inc(s_oh, 1)
                    V_.tensor_scalar(oh_blk[:, n % 4], blocks16[:], part_f[:, 0, k, t:t + 1],
                                     c("token")[:, t:t + 1], ALU.is_equal, ALU.mult).then_inc(s_oh, 1)
                    n += 1
            dve.wait_ge(s_ohu, TILES * TOPK)
            done(V_.tensor_scalar(ids_f[:], ps_unit[:, 0, 0:NBLK], float(ID0), None, ALU.add))
            V_.tensor_copy(ids_i[:], ids_f[:]).then_inc(s_route, 1)

            def gated(b, u):
                dve.wait_ge(s_sg, b + 1)
                if not isinstance(b, int) or b >= 2:
                    dve.wait_ge(s_it, b - 1)
                V_.tensor_tensor(inter[:, u, :], ps_score[:, 1, 2 * u, I:2 * I], sg[:, u, :], ALU.mult).then_inc(s_in, 1)

            def interT_out(b, u):
                dve.wait_ge(s_it, b + 1)
                if not isinstance(b, int) or b >= 2:
                    dve.wait_ge(s_y, b - 1)
                V_.tensor_copy(interT[:, u, :], ps_max[:, u, 0, 0:P]).then_inc(s_ite, 1)

            def y_out(b, u, u4):
                dve.wait_ge(s_y, b + 1)
                if not isinstance(b, int) or b >= 4:
                    dve.wait_ge(s_ys[u4], 4 * (b - u4))
                V_.tensor_copy(yb[:, u4, :], ps_unit[:, u, 0:D]).then_inc(s_ye, 1)

            def blk(k, u4):
                full = not isinstance(k, int)
                if full or 0 <= k - 2 < NBLK:
                    interT_out(k - 2, u4 % 2)
                if full or 0 <= k - 1 < NBLK:
                    gated(k - 1, (u4 - 1) % 2)
                if full or 0 <= k - 3 < NBLK:
                    y_out(k - 3, (u4 - 3) % 2, (u4 - 3) % 4)

            for k in range(8):
                blk(k, k % 4)
            with dve.Fori(0, NBLK // 4 - 2) as trip:
                for u4 in range(4):
                    blk(4 * trip + (8 + u4), u4)
            for k in range(NBLK, NBLK + 3):
                blk(k, k % 4)

            def combine(g, u):
                dve.wait_ge(s_x1b[u], 8 * (g - u) + 16)
                for n in range(0, GT, 2):
                    for k in range(TOPK):
                        for m in (n, n + 1):
                            if k == 0:
                                dve.wait_ge(s_yt[u][m], 16 * (g - u) + 32)
                                if not isinstance(g, int) or g >= 2:
                                    dve.wait_ge(s_o, GT * (g - 2) + m + 1)
                            else:
                                dve.wait_ge(s_z, 2 * GT * g + 2 * n + (m - n) + 1)
                            V_.scalar_tensor_tensor(out=z[:, u, m, :], in0=y_top[:, u, m, k, :],
                                                    scalar=w_top[:, k, bass.ds(GT * g + m, 1)],
                                                    in1=x1b[:, u, m, :] if k == 0 else z[:, u, m, :],
                                                    op0=ALU.mult, op1=ALU.add).then_inc(s_z, 1)
                    for m in (n, n + 1):
                        dve.wait_ge(s_z, 2 * GT * g + 2 * n + 2 + (m - n) + 1)
                        V_.bn_stats(z_stats[:, u, m, :], z[:, u, m, :]).then_inc(s_zs, 1)
                    for m in (n, n + 1):
                        dve.wait_ge(s_zs, GT * g + m + 1)
                        apart(dve)
                        V_.bn_aggr(z_moments[:, u, m, :], z_stats[:, u, m, :]).then_inc(s_zm, 1)

            def final(g, u, first):
                dve.wait_ge(s_zr, g + 1)
                if not first:
                    dve.wait_ge(s_out[u], 8 * (g - u))
                for n in range(GT):
                    V_.tensor_scalar(o[:, u, n, :], z[:, u, n, :], z_moments[:, u, n, 0:1], z_rs[:, u, n:n + 1],
                                     ALU.subtract, ALU.mult).then_inc(s_o, 1)

            combine(0, 0)
            combine(1, 1)
            final(0, 0, True)
            combine(2, 0)
            final(1, 1, True)
            combine(3, 1)
            final(2, 0, False)
            with dve.Fori(0, GROUPS // 2 - 2) as trip:
                for u in range(2):
                    g = 2 * trip + (4 + u)
                    combine(g, u)
                    final(g - 1, 1 - u, False)
            final(GROUPS - 1, 1, False)

        @block.tensor
        def _(pe):
            T = nc.tensor
            ident = c("ident")

            def scores(b, pair, par, first):
                if pair % 2 == 0:
                    pe.wait_ge(s_mrows[pair // 2], 16 * b + 16)
                if not first:
                    pe.wait_ge(s_exp, 8 * b + pair - 1)
                for n in range(2):
                    head = 2 * pair + n
                    for kt in range(ST):
                        mm = T.matmul(ps_score[:, pair % 2, 2 * n + kt, :],
                                      stacks[0:SROWS, par, 1, head // 8, head % 8, kt * P:(kt + 1) * P],
                                      stacks[0:SROWS, par, 0, head // 8, head % 8, :], start=True, stop=True)
                mm.then_inc(s_score, 1)

            def max_scores(b, head, par, first):
                if head % 8 == 0:
                    pe.wait_ge(s_stack[head // 8], 16 * STACK_DMAS * (b + 1))
                if not first:
                    pe.wait_ge(s_red, 16 * b + head - 1)
                for qt in range(ST):
                    mm = T.matmul(ps_max[:, head % 2, qt, :],
                                  stacks[0:QROWS, par, 0, head // 8, head % 8, qt * P:(qt + 1) * P],
                                  stacks[0:QROWS, par, 1, head // 8, head % 8, :], start=True, stop=True)
                mm.then_inc(s_max, 1)

            def fill(i, u, name):
                b, par = i - LAG[name], (u + LAG[name]) % 2
                wait_bank(pe, i, name)
                if name[:2] == "qk":
                    t = int(name[2])
                    pe.wait_ge(s_xqk[par], 8 * (b - par) + 16)
                    for k in range(KC):
                        mm = T.matmul(unit(name), xT_qk[:, par, k, t * P:(t + 1) * P], wqk[:, k, :],
                                      start=(k == 0), stop=(k == KC - 1))
                elif name == "vv":
                    pe.wait_ge(s_xv[par], 8 * (b - par) + 16)
                    for t in range(ST):
                        for k in range(KC):
                            mm = T.matmul(unit(name)[:, t * D:(t + 1) * D], xT_v[:, par, k, t * P:(t + 1) * P],
                                          wv[:, k, :], start=(k == 0), stop=(k == KC - 1))
                elif name[:2] == "tp":
                    l = int(name[2])
                    out4 = unit(name, BF16).rearrange("p (c t) -> p c t", c=4)
                    pe.wait_ge(s_rope, 16 * b + 16)
                    for t in range(ST):
                        for q in range(4):
                            mm = T.transpose(out4[:, q, t * P:(t + 1) * P], planes[:, par, t, l, q * P:(q + 1) * P],
                                             ident16[:])
                elif name[:2] == "mt":
                    g = int(name[2])
                    pe.wait_ge(s_mpl, 4 * b + g + 1)
                    for qt in range(ST):
                        mm = T.transpose(unit(name, BF16)[0:8, qt * P:(qt + 1) * P],
                                         mplanes[:, g, qt].rearrange("p l h -> p (l h)"), ident16[:])
                elif name[:2] == "pv":
                    g = int(name[2])
                    pe.wait_ge(s_exp, 8 * b + 2 * g + 2)
                    was_emptied(pe, b + LAG["vv"], "vv")
                    for kt in range(ST):
                        for n in range(4):
                            pair = 2 * g + n // 2
                            mm = T.matmul(unit(name)[32 * n:32 * n + 32, 0:S], V[:, par, kt, 4 * g + n, :],
                                          probs[:, pair % 4, 2 * (n % 2) + kt, :], start=(kt == 0), stop=(kt == ST - 1))
                elif name[:2] == "tr":
                    t = int(name[2])
                    was_emptied(pe, b + LAG["pv3"], "pv3")
                    for g in range(4):
                        mm = T.transpose(unit(name)[:, g * P:(g + 1) * P], outT[:, par, g, t * P:(t + 1) * P], ident)
                elif name in ("at", "xt"):
                    src = attn if name == "at" else x1[:, par]
                    if name == "at":
                        was_emptied(pe, b + LAG["tr1"], "tr1")
                    else:
                        pe.wait_ge(s_x1, ST * b + ST)
                    for k in range(KC):
                        for t in range(ST):
                            mm = T.transpose(unit(name)[:, k * S + t * P:k * S + (t + 1) * P],
                                             src[:, t, k * P:(k + 1) * P], ident)
                elif name in ("op", "lg"):
                    before, lhs, w, n = ("at", attnT, wo, D) if name == "op" else ("xt", x1T, gw, E)
                    was_emptied(pe, b + LAG[before], before)
                    for t in range(ST):
                        for k in range(KC):
                            mm = T.matmul(unit(name)[:, t * n:(t + 1) * n], lhs[:, k, t * P:(t + 1) * P], w[:, k, :],
                                          start=(k == 0), stop=(k == KC - 1))
                mm.then_inc(filled[name], 1)

            def body(i, u):
                if isinstance(i, int) and i == 1:
                    pe.wait_ge(s_w, 16 * N_W_DMA)
                    pe.wait_ge(s_const, 16)
                    pe.wait_ge(s_setup, 6)
                    pe.wait_ge(s_setup_pool, 3)
                for step in range(8):
                    units = [name for s, name, lag in UNITS if s == step and runs(i, lag)]
                    lag, pair = (3, step + 2) if step < 6 else (2, step - 6)
                    if runs(i, lag):
                        scores(i - lag, pair, (u + lag) % 2, isinstance(i, int) and i == lag == 2)
                    for n in range(max(2, len(units))):
                        if n < 2 and runs(i, 2):
                            max_scores(i - 2, 2 * step + n, u, isinstance(i, int) and i == 2 and step == 0)
                        if n < len(units):
                            fill(i, u, units[n])

            pe.wait_ge(s_wqk, 32)
            iterations(pe, body)

            pe.wait_ge(s_route, 1)
            pos = ps_max[:, 0].rearrange("p t s -> p (t s)")
            T.matmul(pos, before16[:], chosen16[:].rearrange("p t e -> p (t e)"), start=True, stop=False)
            for t in range(TILES - 1):
                after = TILES - 1 - t
                mm = T.matmul(pos[:, (t + 1) * E:].rearrange("p (t e) -> p t e", e=E), ones16[:],
                              chosen16[:, t:t + 1, :].to_broadcast([P, after, E]), start=False, stop=(after == 1))
            mm.then_inc(s_pos, 1)
            for t in range(TILES):
                mm = T.matmul(ps_max[:, 1, 0, 0:E], ones16[:], chosen16[:, t, :], start=(t == 0), stop=(t == TILES - 1))
            mm.then_inc(s_pos, 1)
            for n in range(TILES * TOPK):
                pe.wait_ge(s_oh, 2 * n + 2)
                T.matmul(ps_unit[:, 0, 0:NBLK], oh_in[:, n % 4], oh_blk[:, n % 4], start=(n == 0),
                         stop=(n == TILES * TOPK - 1)).then_inc(s_ohu, 1)

            pe.wait_ge(s_experts, 16 * (KC + 1))

            loaded = {}

            def expert(b):
                return pe.value_load(be_i[0:1, bass.ds(b, 1)], min_val=0, max_val=(E - 1) * D)

            def blk(k, u8):
                full = not isinstance(k, int)
                if full or 0 <= k - 3 < NBLK:
                    w_down = loaded[u8 - 3] if u8 >= 2 and (full or k < NBLK) else expert(k - 3)
                if full or 0 <= k - 1 < NBLK:
                    w_up = loaded[u8 - 1] = expert(k - 1)
                if full or k < NBLK:
                    u = u8 % 2
                    pe.wait_ge(s_xg[u8], 2 * (k - u8) + 16)
                    if full or k >= 2:
                        pe.wait_ge(s_xte, k - 1)
                    for n in range(KC):
                        mm = T.transpose(ps_score[:, 0, 2 * u, n * P:(n + 1) * P], xg[:, u8, n * P:(n + 1) * P], ident)
                    mm.then_inc(s_xt, 1)
                if full or 0 <= k - 1 < NBLK:
                    b, u = k - 1, (u8 - 1) % 2
                    pe.wait_ge(s_xte, b + 1)
                    if full or b >= 2:
                        pe.wait_ge(s_in, b - 1)
                    for n in range(KC):
                        mm = T.matmul(ps_score[:, 1, 2 * u, :], xgT[:, u, n, :],
                                      wgu_flat[:, n, bass.ds(w_up, 2 * I)],
                                      start=(n == 0), stop=(n == KC - 1))
                    mm.then_inc(s_gu, 1)
                if full or 0 <= k - 2 < NBLK:
                    b, u = k - 2, u8 % 2
                    pe.wait_ge(s_in, b + 1)
                    if full or b >= 2:
                        pe.wait_ge(s_ite, b - 1)
                    T.transpose(ps_max[:, u, 0, 0:P], inter[:, u, :], ident).then_inc(s_it, 1)
                if full or 0 <= k - 3 < NBLK:
                    b, u = k - 3, (u8 - 3) % 2
                    pe.wait_ge(s_ite, b + 1)
                    if full or b >= 2:
                        pe.wait_ge(s_ye, b - 1)
                    T.matmul(ps_unit[:, u, 0:D], interT[:, u, :],
                             wdn_flat[:, bass.ds(w_down, D)],
                             start=True, stop=True).then_inc(s_y, 1)

            for k in range(8):
                blk(k, k)
            with pe.Fori(0, NBLK // 8 - 1) as trip:
                for u8 in range(8):
                    blk(8 * trip + (8 + u8), u8)
            for k in range(NBLK, NBLK + 3):
                blk(k, k % 8)


def constants():
    a = np.zeros((P, NCONST), np.float32)

    def put(name, v):
        lo, hi = CONST[name]
        a[:, lo:hi] = np.asarray(v, np.float32).reshape(-1, hi - lo)

    p = np.arange(P)
    put("ident", np.eye(P))
    put("before", p[:, None] < p[None, :])
    inv_freq = (np.float32(1.0) / np.float32(10000.0) ** (np.arange(0, DH, 2, dtype=np.float32) / np.float32(DH)))
    angle = (np.arange(S, dtype=np.float32)[:, None] * inv_freq.astype(np.float32)).astype(np.float32)
    cos, sin = np.cos(angle), np.sin(angle)
    cos = np.concatenate([cos, cos], 1)
    sin = np.concatenate([-sin, sin], 1)
    for name, v in (("cos", cos), ("sin", sin)):
        v = np.repeat(v.reshape(ST, P, DH, 1), 8, axis=3).transpose(1, 0, 2, 3)
        put(name, v.reshape(P, ST * P))
    put("rev", E - np.arange(E))
    put("full", P * np.arange(TILES))
    e = np.arange(E)
    put("lower", e[None, :] < e[:, None])
    put("iota", p)
    put("blocks", np.arange(NBLK))
    put("token", P * np.arange(TILES)[None, :] + p[:, None] - ID0)
    return a


def kernel(L0_attn_x, L0_attn_q_w, L0_attn_k_w, L0_attn_v_w, L0_attn_q_b, L0_attn_k_b, L0_attn_v_b,
           L0_attn_out_w, L0_attn_out_b, L0_ffn_gate_w, L0_ffn_gate_up_proj, L0_ffn_down_proj):
    import concourse.bacc as bacc
    from concourse.bass_utils import run_bass_kernel_spmd

    def arr(v):
        return np.ascontiguousarray(v)

    def by_dim(w):
        w = np.asarray(w)
        return w.reshape(2, 8, DH, -1).transpose(0, 2, 1, 3).reshape(w.shape)

    x = np.asarray(L0_attn_x).reshape(TOK, D)
    bqk = np.concatenate([by_dim(L0_attn_q_b), by_dim(L0_attn_k_b)])
    arrays = {
        "x": arr(x),
        "xT": arr(x.T),
        "wqkT": arr(np.concatenate([by_dim(L0_attn_q_w), by_dim(L0_attn_k_w)]).T),
        "wvT": arr(np.asarray(L0_attn_v_w).T),
        "woT": arr(np.asarray(L0_attn_out_w).T),
        "gateT": arr(np.asarray(L0_ffn_gate_w).T),
        "bqk": arr(np.broadcast_to(bqk, (P, 2 * D))),
        "bv": arr(np.broadcast_to(np.asarray(L0_attn_v_b), (P, D))),
        "bo": arr(np.broadcast_to(np.asarray(L0_attn_out_b), (P, D))),
        "gup": arr(L0_ffn_gate_up_proj),
        "down": arr(L0_ffn_down_proj),
        "const": constants(),
    }
    nc = bacc.Bacc("TRN2", target_bir_lowering=False, num_devices=1)
    args = [nc.dram_tensor(f"in_{name}", a.shape, mybir.dt.from_np(a.dtype), kind="ExternalInput").ap()
            for name, a in arrays.items()]
    out = nc.dram_tensor("out", (TOK, D), F32, kind="ExternalOutput").ap()
    build(nc, *args, out)
    r = run_bass_kernel_spmd(nc, [{f"in_{name}": a for name, a in arrays.items()}], core_ids=[0])
    return r.results[0]["out"].reshape(B, S, D)
```

```python
from contextlib import ExitStack

import concourse.bass as bass
import numpy as np
from concourse import mybir

ALU = mybir.AluOpType
ACT = mybir.ActivationFunctionType
AX = mybir.AxisListType
F32 = mybir.dt.float32
BF16 = mybir.dt.bfloat16
F16 = mybir.dt.float16
I32 = mybir.dt.int32

P = 128
B, S, D = 16, 256, 256
H, DH = 16, 16
E, I, TOPK = 16, 128, 2
TOK = B * S
TILES = TOK // P
KC = D // P
ST = S // P
EPS = 1e-5
SCALE = float(DH) ** -0.5
NBLK = (TOK * TOPK + E * (P - 1)) // P
NBLK += NBLK % 2
ID0 = TOK // 2
GT = 4
GROUPS = TILES // GT
POOL_FROM = 8
OH_TILES = 8
WARM_UP = 8
EARLY = ST * (B - 3)
QROWS = 6 * DH
SROWS = QROWS + 2

CONST = {}
_at = 0
for _name, _n in (("ident", P), ("before", P), ("cos", ST * P), ("sin", ST * P), ("rev", E),
                  ("lower", E * E), ("iota", P), ("blocks", NBLK), ("token", TILES)):
    CONST[_name] = (_at, _at + _n)
    _at += _n
NCONST = _at

UNITS = [
    (0, "qk0", 0), (0, "lg", 5), (0, "mt3", 3),
    (1, "tr0", 4), (1, "tr1", 4), (1, "pv0", 3),
    (2, "at", 4), (2, "pv1", 3), (2, "mt0", 2),
    (3, "tp0", 1), (3, "op", 4),
    (4, "tp1", 1), (4, "qk1", 0), (4, "tp2", 1),
    (5, "mt1", 2), (5, "vv", 2), (5, "pv2", 3),
    (6, "mt2", 2), (6, "pv3", 3),
    (7, "xt", 4),
]
NAMES = [u[1] for u in UNITS]
LAG = {u[1]: u[2] for u in UNITS}
BANK = {name: n % 2 for n, name in enumerate(NAMES)}
MAXLAG = 5
LOOP_FROM, LOOP_TO, ITERATIONS = 6, B - 2, B + MAXLAG


def runs(i, lag):
    return not isinstance(i, int) or 0 <= i - lag < B


def iterations(engine, body):
    for i in range(LOOP_FROM):
        body(i, i % 2)
    with engine.Fori(0, (LOOP_TO - LOOP_FROM) // 2) as trip:
        for u in range(2):
            body(2 * trip + (LOOP_FROM + u), u)
    for i in range(LOOP_TO, ITERATIONS):
        body(i, i % 2)


def build(nc, x, xT, wqkT, wvT, woT, gateT, bqk, bv, bo, gup, down, const, out):
    x_t = x.rearrange("(t p) d -> p t d", p=P)
    out_t = out.rearrange("(t p) d -> p t d", p=P)
    xT_c = xT.rearrange("(c p) t -> p c t", p=P)

    x1_dram = nc.dram_tensor("x1_dram", (TOK, D), F32).ap()
    ys_dram = nc.dram_tensor("ys_dram", (NBLK * P, D), F32).ap()
    x1_t = x1_dram.rearrange("(t p) d -> p t d", p=P)
    ys_t = ys_dram.rearrange("(b p) d -> p b d", p=P)

    with ExitStack() as ctx:
        def sb(name, shape, dt=F32):
            return ctx.enter_context(nc.sbuf_tensor(name, shape, dt))

        def sem(name):
            return ctx.enter_context(nc.semaphore(name))

        cst = sb("cst", [P, NCONST])
        def c(name):
            a, b = CONST[name]
            return cst[:, a:b]
        ident16 = sb("ident16", [P, P], BF16)
        before16 = sb("before16", [P, P], BF16)
        ones16 = sb("ones16", [P, P], BF16)
        iota16 = sb("iota16", [P, P], F16)
        blocks16 = sb("blocks16", [P, NBLK], F16)
        half_neg = sb("half_neg", [P, GT])
        wqk = sb("wqk", [P, KC, 2 * D])
        wv = sb("wv", [P, KC, D])
        wo = sb("wo", [P, KC, D])
        gw = sb("gw", [P, KC, E])
        bqk_sb = sb("bqk_sb", [P, 2 * D])
        bv_sb = sb("bv_sb", [P, D])
        bo_sb = sb("bo_sb", [P, D])

        xT_qk = sb("xT_qk", [P, 2, KC, S])
        xT_v = sb("xT_v", [P, 2, KC, S])
        xn = sb("xn", [P, 2, ST, D])
        xb = sb("xb", [P, ST, D])
        qk = sb("qk", [P, ST, 2 * D])
        rope_a = sb("rope_a", [P, 2 * D])
        rope_b = sb("rope_b", [P, 2 * D])
        planes = sb("planes", [P, 2, ST, 3, 2 * D], BF16)
        planesT = sb("planesT", [P, 4, 3, S], BF16)
        stacks = sb("stacks", [P, 2, 2, 2, 8, S], BF16)
        V = sb("V", [P, 2, ST, H, 32])
        negmax = sb("negmax", [P, ST, H])
        mplanes = sb("mplanes", [P, 4, ST, 2, 4], BF16)
        mT = sb("mT", [8, 4, S], BF16)
        probs = sb("probs", [P, 4, 4, S])
        outT = sb("outT", [P, 2, 4, S])
        inv = sb("inv", [P, ST, H])
        attn = sb("attn", [P, ST, D])
        attnT = sb("attnT", [P, KC, S])
        y = sb("y", [P, ST, D])
        stats = sb("stats", [P, ST, 6])
        moments = sb("moments", [P, ST, 2])
        vareps = sb("vareps", [P, ST])
        rstd = sb("rstd", [P, ST])
        x1 = sb("x1", [P, 2, ST, D])
        x1T = sb("x1T", [P, KC, S])
        logits = sb("logits", [P, TILES, E])

        wgu = sb("wgu", [P, KC, E, 2 * I])
        late = stacks[:].rearrange("p a b c h t -> p (a b c h t)").bitcast(F32)
        wgu_flat = wgu[:].rearrange("p c e f -> p c (e f)")
        wdn_flat = late[:, 0:E * D]
        wdn = wdn_flat.rearrange("p (e h) -> p e h", e=E)
        y_top = late[:, E * D:2 * E * D].rearrange("p (u a k h) -> p u a k h", u=2, a=GT, k=TOPK)
        planes_f = planes[:].rearrange("p u t l n -> p (u t l n)").bitcast(F32)
        R = TILES * E
        r_p, r_a, r_b, r_oh0, r_oh1, r_c = (planes_f[:, n * R:(n + 1) * R].rearrange("p (t e) -> p t e", e=E)
                                            for n in range(6))
        r_oh = (r_oh0, r_oh1)
        probs_f = probs[:].rearrange("p a b s -> p (a b s)")
        x1b = probs_f[:, 0:2 * GT * D].rearrange("p (u a h) -> p u a h", u=2, a=GT)
        o = probs_f[:, 2 * GT * D:4 * GT * D].rearrange("p (u a h) -> p u a h", u=2, a=GT)
        col = sb("col", [P, 8, TILES])
        w_top = sb("w_top", [P, 2, TILES])
        chosen16 = sb("chosen16", [P, TILES, E], BF16)
        running16 = sb("running16", [P, EARLY + 1, E], BF16)
        counts = sb("counts", [P, 4, E])
        slot_f = sb("slot_f", [P, 2, TILES])
        slot_i = sb("slot_i", [P, 2, TILES], I32)
        part_i = sb("part_i", [P, 2, 2, TILES], I32)
        part_f = sb("part_f", [P, 2, TILES])
        base_f = sb("base_f", [P, 2, TILES])
        oh_in = late[:, E * D:2 * E * D].bitcast(F16).rearrange("p (t k n) -> p t k n", t=TILES, k=TOPK)
        oh_blk = probs_f[:, 0:TILES * TOPK * NBLK // 2].bitcast(F16).rearrange("p (t k n) -> p t k n", t=TILES, k=TOPK)
        place_f = sb("place_f", [P, TOPK, TILES])
        block16 = sb("block16", [P, TOPK, TILES], F16)
        ids_f = sb("ids_f", [P, NBLK])
        ids_i = sb("ids_i", [P, NBLK], I32)
        be_f = sb("be_f", [P, 2])
        count_i = sb("count_i", [P, E], I32)
        be_i = sb("be_i", [1, NBLK], I32)
        id_cur = sb("id_cur", [P, 8], I32)
        xg = probs_f[:, 2 * GT * D:2 * GT * D + 8 * D].rearrange("p (a h) -> p a h", a=8)
        xgT = sb("xgT", [P, 2, KC, P])
        sg = sb("sg", [P, 2, I])
        inter = sb("inter", [P, 2, I])
        interT = sb("interT", [P, 2, P])
        yb = sb("yb", [P, 4, D])
        slot_cur = sb("slot_cur", [P, 2, TOPK, GT], I32)
        z = sb("z", [P, 2, GT, D])
        z_stats = sb("z_stats", [P, 2, GT, 6])
        z_moments = sb("z_moments", [P, 2, GT, 2])
        z_var = sb("z_var", [P, 2, GT])
        z_inv = sb("z_inv", [P, 2, GT])
        z_rs = sb("z_rs", [P, 2, GT])

        ps_score = ctx.enter_context(nc.psum_tensor("ps_score", [P, 2, 4, S], F32))
        ps_max = ctx.enter_context(nc.psum_tensor("ps_max", [P, 2, ST, S], F32))
        ps_unit = ctx.enter_context(nc.psum_tensor("ps_unit", [P, 2, 512], F32))

        s_const, s_wqk, s_w, s_experts = (sem("const_loaded"), sem("qk_weights_loaded"), sem("weights_loaded"),
                                          sem("experts_loaded"))
        s_setup, s_setup_pool = sem("setup_vector"), sem("setup_pool")
        s_xqk = [sem(f"xT_qk_loaded{u}") for u in range(2)]
        s_xv = [sem(f"xT_v_loaded{u}") for u in range(2)]
        s_xn = [sem(f"xn_loaded{u}") for u in range(2)]
        s_stack = [sem(f"stack_half_loaded{u}") for u in range(2)]
        s_mrows = [sem(f"max_rows_loaded{g}") for g in range(4)]
        s_x1_out = sem("x1_written")
        filled = {n: sem(f"filled_{n}") for n in NAMES}
        emptied = {n: sem(f"emptied_{n}") for n in NAMES}
        s_score, s_exp = sem("score_pair_filled"), sem("exp_pair_done")
        s_max, s_red = sem("max_head_filled"), sem("max_head_reduced")
        s_mhi, s_mpl = sem("max_high_plane"), sem("max_planes_done")
        s_rope = sem("rope_step")
        s_xb, s_inv = sem("x_with_bias"), sem("sums_inverted")
        s_stats, s_mom, s_ve, s_rstd, s_x1 = (sem("ln_stats"), sem("ln_moments"), sem("ln_var_eps"),
                                             sem("ln_rstd"), sem("x1_done"))
        s_rexp, s_r = sem("router_exp"), sem("router_step")
        s_pos = sem("positions_filled")
        s_chosen, s_running = sem("experts_chosen"), sem("running_sums")
        s_ohin, s_ohin_pool = sem("place_one_hots_done"), sem("place_one_hots_of_pool_done")
        s_ohtok, s_place = sem("one_hots_times_token"), sem("early_places_known")
        s_oh, s_filled_ids = sem("one_hots_done"), sem("ids_filled")
        s_ids, s_be, s_slots = sem("ids_ready"), sem("block_experts_ready"), sem("slots_ready")
        s_idc, s_xg = sem("block_ids_copied"), [sem(f"rows_gathered{u}") for u in range(8)]
        s_xt, s_xte = sem("block_xT_filled"), sem("block_xT_emptied")
        s_gu, s_sg, s_in = sem("gate_up_filled"), sem("gate_silu_done"), sem("inter_done")
        s_it, s_ite = sem("interT_filled"), sem("interT_emptied")
        s_y, s_ye = sem("block_y_filled"), sem("block_y_emptied")
        s_ys = [sem(f"block_y_written{u}") for u in range(4)]
        s_slc, s_yt = sem("slots_copied"), [[sem(f"y_gathered{u}_{n}") for n in range(GT)] for u in range(2)]
        s_x1b = [sem(f"x1_reloaded{u}") for u in range(2)]
        s_warm = sem("silu_table_loaded")
        s_zi, s_zn = sem("z_var_inverted"), sem("z_newton_step")
        s_z, s_zs, s_zm, s_zv, s_zr, s_o = (sem("z_step"), sem("z_stats"), sem("z_moments"), sem("z_var_eps"),
                                            sem("z_rstd"), sem("out_done"))
        s_out = [sem(f"out_written{u}") for u in range(2)]

        def unit(name, dt=F32):
            bank = ps_unit[:, BANK[name], :]
            return bank if dt == F32 else bank.bitcast(dt)

        def wait_bank(pe, i, name):
            n = NAMES.index(name)
            for back in range(1, len(UNITS) * (MAXLAG + 2)):
                m = n - back
                turn = i + (m // len(UNITS))
                other = NAMES[m % len(UNITS)]
                if BANK[other] == BANK[name] and runs(turn, LAG[other]):
                    if isinstance(turn, int) and turn < 0:
                        return
                    pe.wait_ge(emptied[other], turn - LAG[other] + 1)
                    return

        def is_filled(engine, i, name):
            engine.wait_ge(filled[name], i - LAG[name] + 1)

        def was_emptied(engine, i, name):
            engine.wait_ge(emptied[name], i - LAG[name] + 1)

        def apart(engine):
            engine.nop(nofuse=True)

        def position_of(lo, hi):
            bank = (ps_max[:, 0] if lo < EARLY else ps_score[:, 0, 0:2]).rearrange("p t s -> p (t s)")
            return bank[:, 0:TILES * E].rearrange("p (t e) -> p t e", e=E)[:, lo:hi]

        def rope(engine, ops, i, u, t):
            n = 16 * i + 8 * t
            cos = c("cos")[:, t * P:(t + 1) * P].unsqueeze(1).to_broadcast([P, 4, P])
            sin = c("sin")[:, t * P:(t + 1) * P]
            q4 = qk[:, t].rearrange("p (c n) -> p c n", c=4)
            a4 = rope_a[:].rearrange("p (c n) -> p c n", c=4)
            b4 = rope_b[:].rearrange("p (c n) -> p c n", c=4)
            h = P // 2
            if not isinstance(i, int) or n > 0:
                engine.wait_ge(s_rope, n)
            engine.wait_ge(emptied[f"qk{t}"], i + 1)
            ops.tensor_tensor(a4, q4, cos, ALU.mult).then_inc(s_rope, 1)
            for lo, other in ((0, h), (h, 0)):
                ops.tensor_tensor(b4[:, :, lo:lo + h], q4[:, :, other:other + h],
                                  sin[:, lo:lo + h].unsqueeze(1).to_broadcast([P, 4, h]),
                                  ALU.mult).then_inc(s_rope, 1)
            engine.wait_ge(s_rope, n + 3)
            ops.tensor_tensor(rope_a[:], rope_a[:], rope_b[:], ALU.add).then_inc(s_rope, 1)
            if not isinstance(i, int) or i >= 2:
                engine.wait_ge(filled["tp2"], i - 1)
            engine.wait_ge(s_rope, n + 4)
            apart(engine)
            ops.tensor_scalar(planes[:, u, t, 0], rope_a[:], 1.0, 0.0, ALU.mult, ALU.add).then_inc(s_rope, 1)
            engine.wait_ge(s_rope, n + 5)
            ops.tensor_tensor(rope_b[:], rope_a[:], planes[:, u, t, 0], ALU.subtract).then_inc(s_rope, 1)
            engine.wait_ge(s_rope, n + 6)
            apart(engine)
            ops.tensor_scalar(planes[:, u, t, 1], rope_b[:], 1.0, 0.0, ALU.mult, ALU.add).then_inc(s_rope, 1)
            engine.wait_ge(s_rope, n + 7)
            ops.tensor_tensor(planes[:, u, t, 2], rope_b[:], planes[:, u, t, 1], ALU.subtract).then_inc(s_rope, 1)

        N_W_DMA = 5
        STACK_DMAS = 12
        WGU_AT = (0, 0, 4, 5)
        STACK_AT = (0, 3 * DH, 5 * DH)
        X = AX.X

        block = ctx.enter_context(nc.Block())

        @block.sync
        def _(sp):
            sp.dma_start(xT_qk[:, 0], xT_c[:, :, 0:S]).then_inc(s_xqk[0], 16)
            sp.dma_start(wqk[:], wqkT.rearrange("(c p) n -> p c n", p=P)).then_inc(s_wqk, 16)
            sp.dma_start(bqk_sb[:], bqk).then_inc(s_wqk, 16)
            sp.dma_start(cst[:], const).then_inc(s_const, 16)
            for dst, src in ((wv[:], wvT.rearrange("(c p) n -> p c n", p=P)),
                             (wo[:], woT.rearrange("(c p) n -> p c n", p=P)),
                             (gw[:], gateT.rearrange("(c p) n -> p c n", p=P)), (bv_sb[:], bv), (bo_sb[:], bo)):
                sp.dma_start(dst, src).then_inc(s_w, 16)

            def stack_plane(b, u, hh, l):
                for j in range(3 - l):
                    at = STACK_AT[j] + l * DH
                    sp.dma_start(stacks[at:at + DH, u, 0, hh], planesT[:, hh, l, :]).then_inc(s_stack[hh], 16)
                for r in range(3 - l):
                    at = STACK_AT[l] + r * DH
                    sp.dma_start(stacks[at:at + DH, u, 1, hh], planesT[:, 2 + hh, l, :]).then_inc(s_stack[hh], 16)

            def body(i, u):
                if runs(i + 1, 0):
                    if not isinstance(i, int) or i >= 1:
                        sp.wait_ge(filled["qk1"], i)
                    sp.dma_start(xT_qk[:, 1 - u], xT_c[:, :, bass.ds((i + 1) * S, S)]).then_inc(s_xqk[1 - u], 16)
                if runs(i, 1):
                    if not isinstance(i, int) or i >= 3:
                        sp.wait_ge(filled["vv"], i - 2)
                    sp.dma_start(xT_v[:, 1 - u], xT_c[:, :, bass.ds((i - 1) * S, S)]).then_inc(s_xv[1 - u], 16)
                if runs(i, 3):
                    if not isinstance(i, int) or i >= 5:
                        sp.wait_ge(s_xb, i - 4)
                    sp.dma_start(xn[:, 1 - u], x_t[:, bass.ds((i - 3) * ST, ST), :]).then_inc(s_xn[1 - u], 16)
                if isinstance(i, int) and i in WGU_AT:
                    for n, at in enumerate(WGU_AT):
                        if at == i:
                            chunk, e = n // 2, (n % 2) * (E // 2)
                            sp.dma_start(wgu[:, chunk, e:e + E // 2],
                                         gup[e:e + E // 2, chunk * P:(chunk + 1) * P, :].rearrange("e p f -> p e f")
                                         ).then_inc(s_experts, 16)
                if runs(i, 1):
                    for l in range(3):
                        was_emptied(sp, i, f"tp{l}")
                        if l == 0 and runs(i, 3):
                            sp.wait_ge(s_score, 8 * (i - 3) + 4)
                        stack_plane(i - 1, 1 - u, 0, l)
                    if runs(i, 3):
                        sp.wait_ge(s_score, 8 * (i - 3) + 8)
                    for l in range(3):
                        stack_plane(i - 1, 1 - u, 1, l)
                if runs(i, 4):
                    sp.wait_ge(s_x1, ST * (i - 4) + ST)
                    sp.dma_start(x1_t[:, bass.ds((i - 4) * ST, ST), :], x1[:, u]).then_inc(s_x1_out, 16)
                if isinstance(i, int) and i == B + 2:
                    sp.wait_ge(s_score, 8 * B)
                    sp.dma_start(wdn, down.rearrange("e p h -> p e h")).then_inc(s_experts, 16)

            iterations(sp, body)

            with sp.Fori(0, NBLK // 4) as trip:
                for u in range(4):
                    b = 4 * trip + u
                    sp.wait_ge(s_ye, b + 1)
                    sp.dma_start(ys_t[:, bass.ds(b, 1), :], yb[:, u:u + 1, :]).then_inc(s_ys[u], 16)
            def reload(g, u):
                sp.dma_start(x1b[:, u], x1_t[:, bass.ds(GT * g, GT), :]).then_inc(s_x1b[u], 16)

            def store(g, u):
                sp.wait_ge(s_o, GT * g + GT)
                sp.dma_start(out_t[:, bass.ds(GT * g, GT), :], o[:, u]).then_inc(s_out[u], 16)

            sp.wait_ge(s_ids, 1)
            for g in range(2):
                reload(g, g)
            with sp.Fori(0, GROUPS // 2 - 1) as trip:
                for u in range(2):
                    g = 2 * trip + u
                    sp.wait_ge(s_z, 2 * GT * g + 2 * GT)
                    reload(g + 2, u)
                    store(g, u)
            store(GROUPS - 2, 0)
            for n in range(0, GT, 2):
                t = TILES - GT + n
                sp.wait_ge(s_o, t + 2)
                sp.dma_start(out_t[:, t:t + 2, :], o[:, 1, n:n + 2]).then_inc(s_out[1], 16)
            sp.wait_ge(s_out[0], 16 * GROUPS // 2)
            sp.wait_ge(s_out[1], 16 * (GROUPS // 2 - 1 + GT // 2))

        @block.gpsimd
        def _(pool):
            pool.memset(half_neg[:], -0.5).then_inc(s_setup_pool, 1)
            pool.memset(V[:], 0.0).then_inc(s_setup_pool, 1)
            pool.wait_ge(s_setup_pool, 2)
            pool.memset(V[:, :, :, :, DH:DH + 1], 1.0).then_inc(s_setup_pool, 1)
            pool.wait_ge(s_const, 16)
            pool.wait_ge(s_w, 16 * N_W_DMA)

            def running_sums():
                pool.memset(running16[:, 0], 0.0).then_inc(s_running, 1)
                pool.wait_ge(s_chosen, 1)
                for t in range(EARLY):
                    pool.wait_ge(s_running, t + 1)
                    pool.tensor_tensor(running16[:, t + 1], running16[:, t], chosen16[:, t], ALU.add).then_inc(s_running, 1)

            def body(i, u):
                if runs(i, 4):
                    b = i - 4
                    pool.wait_ge(s_xn[u], 8 * (b - u) + 16)
                    if not isinstance(i, int) or i >= 5:
                        pool.wait_ge(emptied["op"], b)
                    pool.tensor_tensor(xb[:], xn[:, u], bo_sb[:].unsqueeze(1).to_broadcast([P, ST, D]),
                                       ALU.add).then_inc(s_xb, 1)
                if isinstance(i, int) and i == B + 3:
                    running_sums()
                if runs(i, 0) and not (isinstance(i, int) and i == 0):
                    rope(pool, pool, i, u, 0)
                if runs(i, 4):
                    pool.wait_ge(s_mom, ST * b + ST)
                    apart(pool)
                    pool.tensor_scalar(vareps[:], moments[:, :, 1], 1.0, EPS, ALU.mult, ALU.add).then_inc(s_ve, 1)
                    pool.wait_ge(s_ve, b + 1)
                    pool.tensor_tensor(rstd[:], vareps[:], half_neg[:, 0:ST], ALU.pow).then_inc(s_rstd, 1)
                if runs(i, 0) and not (isinstance(i, int) and i == 0):
                    rope(pool, pool, i, u, 1)

            iterations(pool, body)

            pool.wait_ge(s_place, 1)
            for t in range(POOL_FROM, EARLY):
                for k in range(TOPK):
                    apart(pool)
                    ins = pool.tensor_scalar(oh_in[:, t, k], iota16[:], place_f[:, k, t:t + 1], None, ALU.is_equal)
                ins.then_inc(s_ohin_pool, 1)
            pool.wait_ge(s_x1_out, 16 * B)
            pool.wait_ge(s_ids, 1)

            def gather(b, u, group, first):
                if u % 4 == 0:
                    pool.wait_ge(s_idc, group + 1)
                if not first:
                    pool.wait_ge(s_xt, b - 7)
                apart(pool)
                pool.indirect_dma_start(out=xg[:, u, :], out_offset=None, in_=x1_dram,
                                        in_offset=bass.IndirectOffsetOnAxis(ap=id_cur[:, u:u + 1], axis=0)
                                        ).then_inc(s_xg[u], 16)

            for u in range(8):
                gather(u, u, u // 4, True)
            with pool.Fori(0, NBLK // 8 - 1) as trip:
                for u in range(8):
                    gather(8 * trip + (8 + u), u, 2 * trip + (2 + u // 4), False)
            for u in range(4):
                pool.wait_ge(s_ys[u], 16 * NBLK // 4)

            def top(g, u, first):
                pool.wait_ge(s_slc, g + 1)
                for n in range(GT):
                    if not first:
                        pool.wait_ge(s_z, 2 * GT * (g - 2) + 4 * (n // 2) + 4)
                    for k in range(TOPK):
                        apart(pool)
                        pool.indirect_dma_start(out=y_top[:, u, n, k, :], out_offset=None, in_=ys_dram,
                                                in_offset=bass.IndirectOffsetOnAxis(ap=slot_cur[:, u, k, n:n + 1], axis=0)
                                                ).then_inc(s_yt[u][n], 16)

            top(0, 0, True)
            top(1, 1, True)
            with pool.Fori(0, GROUPS // 2 - 1) as trip:
                for u in range(2):
                    top(2 * trip + (2 + u), u, False)

        @block.scalar
        def _(act):
            def empty(i, name, dst, src):
                is_filled(act, i, name)
                nc.scalar.copy(dst, src).then_inc(emptied[name], 1)

            def exp(b, pair, first):
                slot = pair % 4
                act.wait_ge(s_score, 8 * b + pair + 1)
                if pair >= 4:
                    act.wait_ge(filled[f"pv{(pair - 4) // 2}"], b + 1)
                elif not first:
                    act.wait_ge(filled[f"pv{(pair + 4) // 2}"], b)
                nc.scalar.activation(probs[:, slot], ps_score[:, pair % 2], ACT.Exp, scale=SCALE).then_inc(s_exp, 1)

            def body(i, u):
                if isinstance(i, int) and i == B + 1:
                    router_exp(0, EARLY)
                for step in range(8):
                    lag, pair = (3, step + 2) if step < 6 else (2, step - 6)
                    if runs(i, lag):
                        exp(i - lag, pair, isinstance(i, int) and i == lag)
                    for s, name, ulag in UNITS:
                        if s != step or not runs(i, ulag):
                            continue
                        if name[:2] == "pv":
                            g = int(name[2])
                            if not isinstance(i, int) or i >= 5:
                                act.wait_ge(filled["tr1"], i - 4)
                            empty(i, name, outT[:, 1 - u, g, :], unit(name)[:, 0:S])
                        elif name[:2] == "mt":
                            g = int(name[2])
                            empty(i, name, mT[:, g, :], unit(name, BF16)[0:8, 0:S])
                            was_emptied(act, i, name)
                            act.dma_start(stacks[QROWS:SROWS, (u + ulag) % 2, 0, g // 2, 4 * (g % 2):4 * (g % 2) + 4, :],
                                          mT[:, g, :]).then_inc(s_mrows[g], 16)
                        elif name[:2] == "tp":
                            l = int(name[2])
                            if not isinstance(i, int) or i >= 2:
                                for half in s_stack:
                                    act.wait_ge(half, 16 * STACK_DMAS * (i - 1))
                            empty(i, name, planesT[:, :, l, :], unit(name, BF16).rearrange("p (c t) -> p c t", c=4))
                        elif name == "at":
                            empty(i, name, attnT[:], unit(name).rearrange("p (c t) -> p c t", c=KC))
                        elif name == "xt":
                            empty(i, name, x1T[:], unit(name).rearrange("p (c t) -> p c t", c=KC))

            def router_exp(lo, hi):
                act.wait_ge(emptied["lg"], hi // ST)
                nc.scalar.activation(r_p[:, lo:hi], logits[:, lo:hi], ACT.Exp, scale=-1.0).then_inc(s_rexp, 1)

            def times_token():
                for t in range(TILES):
                    if POOL_FROM <= t < EARLY:
                        act.wait_ge(s_ohin_pool, t - POOL_FROM + 1)
                    else:
                        act.wait_ge(s_ohin, t + 1 if t < EARLY else t + 1 - (EARLY - POOL_FROM))
                    nc.scalar.activation(oh_in[:, t], oh_in[:, t], ACT.Copy, scale=c("token")[:, t:t + 1]).then_inc(s_ohtok, 1)

            iterations(act, body)
            router_exp(EARLY, TILES)
            times_token()
            nc.scalar.activation(sg[:, 0, 0:1], half_neg[:, 0:1], ACT.Silu).then_inc(s_warm, 1)
            act.wait_ge(s_warm, 1)

            act.wait_ge(s_ids, 1)

            def ids_copy(g, h):
                nc.scalar.copy(id_cur[:, 4 * h:4 * h + 4], ids_i[:, bass.ds(4 * g, 4)]).then_inc(s_idc, 1)

            def xT_out(b, u):
                act.wait_ge(s_xt, b + 1)
                if not isinstance(b, int) or b >= 2:
                    act.wait_ge(s_gu, b - 1)
                nc.scalar.copy(xgT[:, u].rearrange("p c t -> p (c t)"), ps_score[:, 0, 2 * u, :]).then_inc(s_xte, 1)

            def silu(b, u):
                act.wait_ge(s_gu, b + 1)
                if not isinstance(b, int) or b >= 2:
                    act.wait_ge(s_in, b - 1)
                nc.scalar.activation(sg[:, u, :], ps_score[:, 1, 2 * u, 0:P], ACT.Silu).then_inc(s_sg, 1)

            def blk(k, u8, trip8):
                full = not isinstance(k, int)
                if u8 % 4 == 0 and (full or k + 4 < NBLK) and (full or k > 0):
                    ids_copy(2 * trip8 + (u8 // 4 + 1), (u8 // 4 + 1) % 2)
                if full or k < NBLK:
                    xT_out(k, u8 % 2)
                if full or 0 <= k - 1 < NBLK:
                    silu(k - 1, (u8 - 1) % 2)

            ids_copy(0, 0)
            ids_copy(1, 1)
            for k in range(8):
                blk(k, k, 0)
            with act.Fori(0, NBLK // 8 - 2) as trip:
                for u8 in range(8):
                    blk(8 * trip + (8 + u8), u8, trip + 1)
            for k in range(NBLK - 8, NBLK + 1):
                blk(k, k % 8, k // 8)

            def slots_copy(g, u, first):
                if not first:
                    act.wait_ge(s_z, 2 * GT * (g - 1))
                nc.scalar.copy(slot_cur[:, u], slot_i[:, :, bass.ds(GT * g, GT)]).then_inc(s_slc, 1)

            act.wait_ge(s_slots, 1)
            def z_root(g, u):
                act.wait_ge(s_zi, g + 1)
                nc.scalar.activation(z_rs[:, u], z_inv[:, u], ACT.Sqrt).then_inc(s_zr, 1)

            slots_copy(0, 0, True)
            slots_copy(1, 1, True)
            with act.Fori(0, GROUPS // 2 - 1) as trip:
                for u in range(2):
                    z_root(2 * trip + u, u)
                    slots_copy(2 * trip + (2 + u), u, False)
            for u in range(2):
                z_root(GROUPS - 2 + u, u)

        @block.vector
        def _(dve):
            V_ = nc.vector
            V_.memset(ones16[:], 1.0).then_inc(s_setup, 1)
            pair = float(np.array([0x3F803F80], np.uint32).view(np.float32)[0])
            k_rows = stacks[QROWS:P, :, 1].rearrange("p a c h t -> p a (c h t)").bitcast(F32)
            V_.memset(k_rows, pair).then_inc(s_setup, 1)
            dve.wait_ge(s_const, 16)
            V_.tensor_copy(ident16[:], c("ident")).then_inc(s_setup, 1)
            V_.tensor_copy(before16[:], c("before")).then_inc(s_setup, 1)
            V_.tensor_copy(iota16[:], c("iota")).then_inc(s_setup, 1)
            V_.tensor_copy(blocks16[:], c("blocks")).then_inc(s_setup, 1)
            dve.wait_ge(s_wqk, 32)
            dve.wait_ge(s_w, 16 * N_W_DMA)
            dve.wait_ge(s_setup_pool, 3)

            def reduce_head(b, h):
                dve.wait_ge(s_max, 16 * b + h + 1)
                V_.tensor_reduce(negmax[:, :, h], ps_max[:, h % 2], X, ALU.max, negate=True).then_inc(s_red, 1)

            def max_planes(b, g):
                dve.wait_ge(s_red, 16 * b + 4 * g + 4)
                m = negmax[:, :, 4 * g:4 * g + 4]
                V_.tensor_copy(mplanes[:, g, :, 0, :], m).then_inc(s_mhi, 1)
                dve.wait_ge(s_mhi, 4 * b + g + 1)
                V_.tensor_tensor(mplanes[:, g, :, 1, :], m, mplanes[:, g, :, 0, :], ALU.subtract).then_inc(s_mpl, 1)

            def unit_out(i, u, name):
                b = i - LAG[name]
                is_filled(dve, i, name)
                if name[:2] == "qk":
                    t = int(name[2])
                    if not isinstance(i, int) or i >= 1:
                        dve.wait_ge(s_rope, 16 * (b - 1) + 8 * t + 3)
                    V_.tensor_tensor(qk[:, t], unit(name), bqk_sb[:], ALU.add).then_inc(emptied[name], 1)
                elif name == "vv":
                    V_.tensor_tensor(V[:, u, :, :, 0:DH], unit(name).rearrange("p (t h d) -> p t h d", t=ST, h=H),
                                     bv_sb[:].rearrange("p (h d) -> p h d", h=H).unsqueeze(1).to_broadcast([P, ST, H, DH]),
                                     ALU.add).then_inc(emptied[name], 1)
                elif name[:2] == "tr":
                    t = int(name[2])
                    r = unit(name).rearrange("p (h j) -> p h j", j=32)
                    V_.reciprocal(inv[:, t, :], r[:, :, DH:DH + 1].rearrange("p h j -> p (h j)")).then_inc(s_inv, 1)
                    dve.wait_ge(s_inv, ST * b + t + 1)
                    V_.tensor_tensor(attn[:, t].rearrange("p (h d) -> p h d", h=H), r[:, :, 0:DH],
                                     inv[:, t, :].unsqueeze(2).to_broadcast([P, H, DH]), ALU.mult).then_inc(emptied[name], 1)
                elif name == "op":
                    dve.wait_ge(s_xb, b + 1)
                    V_.tensor_tensor(y[:], unit(name).rearrange("p (t d) -> p t d", t=ST), xb[:],
                                     ALU.add).then_inc(emptied[name], 1)
                    was_emptied(dve, i, "op")
                    for t in range(ST):
                        V_.bn_stats(stats[:, t, :], y[:, t, :]).then_inc(s_stats, 1)
                    for t in range(ST):
                        dve.wait_ge(s_stats, ST * b + t + 1)
                        apart(dve)
                        V_.bn_aggr(moments[:, t, :], stats[:, t, :]).then_inc(s_mom, 1)
                elif name == "lg":
                    V_.tensor_copy(logits[:, bass.ds(b * ST, ST), :],
                                   unit(name)[:, 0:ST * E].rearrange("p (t e) -> p t e", t=ST)).then_inc(emptied[name], 1)

            def normalise(b, u, first):
                dve.wait_ge(s_rstd, b + 1)
                if not first:
                    dve.wait_ge(s_x1_out, 16 * (b - 1))
                    dve.wait_ge(filled["xt"], b - 1)
                for t in range(ST):
                    V_.tensor_scalar(x1[:, u, t, :], y[:, t, :], moments[:, t, 0:1], rstd[:, t:t + 1],
                                     ALU.subtract, ALU.mult).then_inc(s_x1, 1)

            def body(i, u):
                for step in range(8):
                    units = [name for s, name, lag in UNITS if s == step and runs(i, lag)]
                    for n in range(max(2, len(units))):
                        if n < 2 and runs(i, 2):
                            reduce_head(i - 2, 2 * step + n)
                            if n == 1 and step % 2:
                                max_planes(i - 2, step // 2)
                        if n < len(units) and units[n][:2] in ("qk", "vv", "tr", "op", "lg"):
                            unit_out(i, u, units[n])
                            if isinstance(i, int) and i == 0:
                                rope(dve, V_, 0, 0, int(units[n][2]))
                    if step == 5 and runs(i, 4):
                        normalise(i - 4, u, isinstance(i, int) and i < 6)
                    if isinstance(i, int):
                        early_routing(i, step)

            step_no = [0]

            def done(ins):
                step_no[0] += 1
                ins.then_inc(s_r, 1)
                dve.wait_ge(s_r, step_no[0])

            def row(n, lo, hi):
                return col[:, n, lo:hi]

            def over_e(a, n):
                return a.unsqueeze(2).to_broadcast([P, n, E])

            def router_probs(lo, hi):
                dve.wait_ge(s_rexp, 1 if lo == 0 else 2)
                done(V_.tensor_scalar(r_a[:, lo:hi], r_p[:, lo:hi], 1.0, None, ALU.add))
                done(V_.reciprocal(r_b[:, lo:hi], r_a[:, lo:hi]))
                done(V_.reduce_sum(row(0, lo, hi), r_b[:, lo:hi], X))
                done(V_.reciprocal(row(1, lo, hi), row(0, lo, hi)))
                done(V_.tensor_tensor(r_p[:, lo:hi], r_b[:, lo:hi], over_e(row(1, lo, hi), hi - lo), ALU.mult))

            def choose(lo, hi, k):
                rev = c("rev").unsqueeze(1).to_broadcast([P, hi - lo, E])
                done(V_.tensor_reduce(row(2 + k, lo, hi), r_p[:, lo:hi], X, ALU.max))
                done(V_.tensor_tensor(r_a[:, lo:hi], r_p[:, lo:hi], over_e(row(2 + k, lo, hi), hi - lo), ALU.is_equal))
                done(V_.tensor_tensor(r_b[:, lo:hi], r_a[:, lo:hi], rev, ALU.mult))
                done(V_.tensor_reduce(row(4, lo, hi), r_b[:, lo:hi], X, ALU.max))
                done(V_.tensor_tensor(r_oh[k][:, lo:hi], rev, over_e(row(4, lo, hi), hi - lo), ALU.is_equal))
                if k == 0:
                    done(V_.scalar_tensor_tensor(out=r_p[:, lo:hi], in0=r_oh[0][:, lo:hi], scalar=-4.0,
                                                 in1=r_p[:, lo:hi], op0=ALU.mult, op1=ALU.add))
                else:
                    V_.tensor_tensor(chosen16[:, lo:hi], r_oh[0][:, lo:hi], r_oh[1][:, lo:hi], ALU.add).then_inc(s_chosen, 1)

            def places(lo, hi):
                n = hi - lo
                dve.wait_ge(s_pos, 1 if lo == 0 else 3)
                pos = position_of(lo, hi)
                V_.tensor_tensor(r_a[:, lo:hi], pos, r_oh[0][:, lo:hi], ALU.mult).then_inc(s_r, 1)
                V_.tensor_tensor(r_b[:, lo:hi], pos, r_oh[1][:, lo:hi], ALU.mult).then_inc(s_r, 1)
                step_no[0] += 2
                dve.wait_ge(s_r, step_no[0])
                V_.reduce_sum(slot_f[:, 0, lo:hi], r_a[:, lo:hi], X).then_inc(s_r, 1)
                V_.reduce_sum(slot_f[:, 1, lo:hi], r_b[:, lo:hi], X).then_inc(s_r, 1)
                step_no[0] += 2
                dve.wait_ge(s_r, step_no[0])
                done(V_.tensor_copy(slot_i[:, :, lo:hi], slot_f[:, :, lo:hi]))
                V_.tensor_scalar(part_i[:, 0, :, lo:hi], slot_i[:, :, lo:hi], 7, None, ALU.arith_shift_right).then_inc(s_r, 1)
                V_.tensor_scalar(part_i[:, 1, :, lo:hi], slot_i[:, :, lo:hi], P - 1, None, ALU.bitwise_and).then_inc(s_r, 1)
                step_no[0] += 2
                dve.wait_ge(s_r, step_no[0])
                V_.tensor_copy(place_f[:, :, lo:hi], part_i[:, 1, :, lo:hi]).then_inc(s_r, 1)
                step_no[0] += 1
                done(V_.tensor_copy(part_f[:, :, lo:hi], part_i[:, 0, :, lo:hi]))

            def place_one_hots(lo, hi):
                for t in range(lo, hi):
                    for k in range(TOPK):
                        ins = V_.tensor_scalar(oh_in[:, t, k], iota16[:], place_f[:, k, t:t + 1], None, ALU.is_equal)
                    ins.then_inc(s_ohin, 1)

            def early_routing(i, step):
                if (i, step) == (B + 1, 7):
                    router_probs(0, EARLY)
                elif (i, step) == (B + 2, 1):
                    choose(0, EARLY, 0)
                elif (i, step) == (B + 2, 5):
                    choose(0, EARLY, 1)
                elif (i, step) == (B + 3, 5):
                    places(0, EARLY)
                    dve.wait_ge(s_score, 8 * B)
                    dve.nop(nofuse=True).then_inc(s_place, 1)
                    place_one_hots(0, POOL_FROM)

            iterations(dve, body)

            router_probs(EARLY, TILES)
            choose(EARLY, TILES, 0)
            choose(EARLY, TILES, 1)
            dve.wait_ge(s_pos, 2)
            done(V_.tensor_scalar(count_i[:], ps_max[:, 1, 0, 0:E], float(P - 1), None, ALU.add))
            done(V_.tensor_scalar(count_i[:], count_i[:], 7, None, ALU.arith_shift_right))
            done(V_.tensor_copy(counts[:, 0, :], count_i[:]))
            places(EARLY, TILES)
            place_one_hots(EARLY, TILES)
            low = r_c[:, 0:E]
            done(V_.tensor_tensor(low, counts[:, 0, :].unsqueeze(1).to_broadcast([P, E, E]),
                                  c("lower").rearrange("p (e f) -> p e f", e=E), ALU.mult))
            done(V_.reduce_sum(counts[:, 1, :], low, X))
            done(V_.tensor_tensor(counts[:, 2, :], counts[:, 0, :], counts[:, 1, :], ALU.add))
            done(V_.tensor_scalar(counts[:, 3, :], counts[:, 2, :], c("token")[:, ID0 // P:ID0 // P + 1], None, ALU.is_le))
            done(V_.reduce_sum(be_f[:, 0:1], counts[:, 3, :], X))
            V_.tensor_scalar(be_f[:, 1:2], be_f[:, 0:1], float(E - 1), float(D), ALU.min, ALU.mult).then_inc(s_be, 1)
            before = counts[:, 1, :].unsqueeze(1).to_broadcast([P, TILES, E])
            V_.tensor_tensor(r_a, before, r_oh[0], ALU.mult).then_inc(s_r, 1)
            V_.tensor_tensor(r_b, before, r_oh[1], ALU.mult).then_inc(s_r, 1)
            step_no[0] += 2
            dve.wait_ge(s_r, step_no[0])
            V_.reduce_sum(base_f[:, 0, :], r_a, X).then_inc(s_r, 1)
            V_.reduce_sum(base_f[:, 1, :], r_b, X).then_inc(s_r, 1)
            step_no[0] += 2
            dve.wait_ge(s_r, step_no[0])
            done(V_.tensor_tensor(block16[:], part_f[:], base_f[:], ALU.add))
            for lo in range(0, TILES, OH_TILES):
                for k in range(TOPK):
                    ins = V_.tensor_tensor(oh_blk[:, lo:lo + OH_TILES, k],
                                           blocks16[:].unsqueeze(1).to_broadcast([P, OH_TILES, NBLK]),
                                           block16[:, k, lo:lo + OH_TILES].unsqueeze(2).to_broadcast([P, OH_TILES, NBLK]),
                                           ALU.is_equal)
                ins.then_inc(s_oh, 1)
            dve.wait_ge(s_be, 2)
            V_.tensor_copy(be_i[:], ps_score[0:1, 1, 0, 0:NBLK]).then_inc(s_be, 1)
            dve.wait_ge(s_filled_ids, 1)
            done(V_.tensor_scalar(ids_f[:], ps_unit[:, 0, 0:NBLK], float(ID0), None, ALU.add))
            V_.tensor_copy(ids_i[:], ids_f[:]).then_inc(s_ids, 1)
            done(V_.scalar_tensor_tensor(out=slot_f[:], in0=base_f[:], scalar=float(P), in1=slot_f[:],
                                         op0=ALU.mult, op1=ALU.add))
            V_.tensor_copy(slot_i[:], slot_f[:]).then_inc(s_slots, 1)
            done(V_.tensor_tensor(col[:, 5], col[:, 2], col[:, 3], ALU.add))
            done(V_.reciprocal(col[:, 6], col[:, 5]))
            for k in range(TOPK):
                done(V_.tensor_tensor(w_top[:, k, :], col[:, 2 + k], col[:, 6], ALU.mult))

            def gated(b, u):
                dve.wait_ge(s_sg, b + 1)
                if not isinstance(b, int) or b >= 2:
                    dve.wait_ge(s_it, b - 1)
                V_.tensor_tensor(inter[:, u, :], ps_score[:, 1, 2 * u, I:2 * I], sg[:, u, :], ALU.mult).then_inc(s_in, 1)

            def interT_out(b, u):
                dve.wait_ge(s_it, b + 1)
                if not isinstance(b, int) or b >= 2:
                    dve.wait_ge(s_y, b - 1)
                V_.tensor_copy(interT[:, u, :], ps_max[:, u, 0, 0:P]).then_inc(s_ite, 1)

            def y_out(b, u, u4):
                dve.wait_ge(s_y, b + 1)
                if not isinstance(b, int) or b >= 4:
                    dve.wait_ge(s_ys[u4], 4 * (b - u4))
                V_.tensor_copy(yb[:, u4, :], ps_unit[:, u, 0:D]).then_inc(s_ye, 1)

            def blk(k, u4):
                full = not isinstance(k, int)
                if full or 0 <= k - 2 < NBLK:
                    interT_out(k - 2, u4 % 2)
                if full or 0 <= k - 1 < NBLK:
                    gated(k - 1, (u4 - 1) % 2)
                if full or 0 <= k - 3 < NBLK:
                    y_out(k - 3, (u4 - 3) % 2, (u4 - 3) % 4)

            for k in range(8):
                blk(k, k % 4)
            with dve.Fori(0, NBLK // 4 - 2) as trip:
                for u4 in range(4):
                    blk(4 * trip + (8 + u4), u4)
            for k in range(NBLK, NBLK + 3):
                blk(k, k % 4)

            def combine(g, u):
                dve.wait_ge(s_x1b[u], 8 * (g - u) + 16)
                for n in range(0, GT, 2):
                    for k in range(TOPK):
                        for m in (n, n + 1):
                            if k == 0:
                                dve.wait_ge(s_yt[u][m], 16 * (g - u) + 32)
                                if not isinstance(g, int) or g >= 2:
                                    dve.wait_ge(s_o, GT * (g - 2) + m + 1)
                            else:
                                dve.wait_ge(s_z, 2 * GT * g + 2 * n + (m - n) + 1)
                            V_.scalar_tensor_tensor(out=z[:, u, m, :], in0=y_top[:, u, m, k, :],
                                                    scalar=w_top[:, k, bass.ds(GT * g + m, 1)],
                                                    in1=x1b[:, u, m, :] if k == 0 else z[:, u, m, :],
                                                    op0=ALU.mult, op1=ALU.add).then_inc(s_z, 1)
                    for m in (n, n + 1):
                        dve.wait_ge(s_z, 2 * GT * g + 2 * n + 2 + (m - n) + 1)
                        V_.bn_stats(z_stats[:, u, m, :], z[:, u, m, :]).then_inc(s_zs, 1)
                    for m in (n, n + 1):
                        dve.wait_ge(s_zs, GT * g + m + 1)
                        apart(dve)
                        V_.bn_aggr(z_moments[:, u, m, :], z_stats[:, u, m, :]).then_inc(s_zm, 1)
                dve.wait_ge(s_zm, GT * g + GT)
                V_.tensor_scalar(z_var[:, u], z_moments[:, u, :, 1], EPS, None, ALU.add).then_inc(s_zv, 1)
                dve.wait_ge(s_zv, g + 1)
                V_.reciprocal(z_inv[:, u], z_var[:, u]).then_inc(s_zi, 1)

            def final(g, u, first):
                dve.wait_ge(s_zr, g + 1)
                r, v, w = z_rs[:, u], z_var[:, u], z_inv[:, u]
                V_.scalar_tensor_tensor(out=w, in0=r, scalar=-0.5, in1=r, op0=ALU.mult, op1=ALU.mult).then_inc(s_zn, 1)
                dve.wait_ge(s_zn, 3 * g + 1)
                V_.tensor_tensor(w, w, v, ALU.mult).then_inc(s_zn, 1)
                dve.wait_ge(s_zn, 3 * g + 2)
                V_.scalar_tensor_tensor(out=r, in0=w, scalar=1.5, in1=r, op0=ALU.add, op1=ALU.mult).then_inc(s_zn, 1)
                dve.wait_ge(s_zn, 3 * g + 3)
                if not first:
                    dve.wait_ge(s_out[u], 8 * (g - u))
                for n in range(GT):
                    V_.tensor_scalar(o[:, u, n, :], z[:, u, n, :], z_moments[:, u, n, 0:1], z_rs[:, u, n:n + 1],
                                     ALU.subtract, ALU.mult).then_inc(s_o, 1)

            combine(0, 0)
            combine(1, 1)
            final(0, 0, True)
            combine(2, 0)
            final(1, 1, True)
            combine(3, 1)
            final(2, 0, False)
            with dve.Fori(0, GROUPS // 2 - 2) as trip:
                for u in range(2):
                    g = 2 * trip + (4 + u)
                    combine(g, u)
                    final(g - 1, 1 - u, False)
            final(GROUPS - 1, 1, False)

        @block.tensor
        def _(pe):
            T = nc.tensor
            ident = c("ident")

            def scores(b, pair, par, first):
                if pair % 2 == 0:
                    pe.wait_ge(s_mrows[pair // 2], 16 * b + 16)
                if not first:
                    pe.wait_ge(s_exp, 8 * b + pair - 1)
                for n in range(2):
                    head = 2 * pair + n
                    for kt in range(ST):
                        mm = T.matmul(ps_score[:, pair % 2, 2 * n + kt, :],
                                      stacks[0:SROWS, par, 1, head // 8, head % 8, kt * P:(kt + 1) * P],
                                      stacks[0:SROWS, par, 0, head // 8, head % 8, :], start=True, stop=True)
                mm.then_inc(s_score, 1)

            def max_scores(b, head, par, first):
                if head % 8 == 0:
                    pe.wait_ge(s_stack[head // 8], 16 * STACK_DMAS * (b + 1))
                if not first:
                    pe.wait_ge(s_red, 16 * b + head - 1)
                for qt in range(ST):
                    mm = T.matmul(ps_max[:, head % 2, qt, :],
                                  stacks[0:QROWS, par, 0, head // 8, head % 8, qt * P:(qt + 1) * P],
                                  stacks[0:QROWS, par, 1, head // 8, head % 8, :], start=True, stop=True)
                mm.then_inc(s_max, 1)

            def fill(i, u, name):
                b, par = i - LAG[name], (u + LAG[name]) % 2
                wait_bank(pe, i, name)
                if name[:2] == "qk":
                    t = int(name[2])
                    pe.wait_ge(s_xqk[par], 8 * (b - par) + 16)
                    for k in range(KC):
                        mm = T.matmul(unit(name), xT_qk[:, par, k, t * P:(t + 1) * P], wqk[:, k, :],
                                      start=(k == 0), stop=(k == KC - 1))
                elif name == "vv":
                    pe.wait_ge(s_xv[par], 8 * (b - par) + 16)
                    for t in range(ST):
                        for k in range(KC):
                            mm = T.matmul(unit(name)[:, t * D:(t + 1) * D], xT_v[:, par, k, t * P:(t + 1) * P],
                                          wv[:, k, :], start=(k == 0), stop=(k == KC - 1))
                elif name[:2] == "tp":
                    l = int(name[2])
                    out4 = unit(name, BF16).rearrange("p (c t) -> p c t", c=4)
                    pe.wait_ge(s_rope, 16 * b + 16)
                    for t in range(ST):
                        for q in range(4):
                            mm = T.transpose(out4[:, q, t * P:(t + 1) * P], planes[:, par, t, l, q * P:(q + 1) * P],
                                             ident16[:])
                elif name[:2] == "mt":
                    g = int(name[2])
                    pe.wait_ge(s_mpl, 4 * b + g + 1)
                    for qt in range(ST):
                        mm = T.transpose(unit(name, BF16)[0:8, qt * P:(qt + 1) * P],
                                         mplanes[:, g, qt].rearrange("p l h -> p (l h)"), ident16[:])
                elif name[:2] == "pv":
                    g = int(name[2])
                    pe.wait_ge(s_exp, 8 * b + 2 * g + 2)
                    was_emptied(pe, b + LAG["vv"], "vv")
                    for kt in range(ST):
                        for n in range(4):
                            pair = 2 * g + n // 2
                            mm = T.matmul(unit(name)[32 * n:32 * n + 32, 0:S], V[:, par, kt, 4 * g + n, :],
                                          probs[:, pair % 4, 2 * (n % 2) + kt, :], start=(kt == 0), stop=(kt == ST - 1))
                elif name[:2] == "tr":
                    t = int(name[2])
                    was_emptied(pe, b + LAG["pv3"], "pv3")
                    for g in range(4):
                        mm = T.transpose(unit(name)[:, g * P:(g + 1) * P], outT[:, par, g, t * P:(t + 1) * P], ident)
                elif name in ("at", "xt"):
                    src = attn if name == "at" else x1[:, par]
                    if name == "at":
                        was_emptied(pe, b + LAG["tr1"], "tr1")
                    else:
                        pe.wait_ge(s_x1, ST * b + ST)
                    for k in range(KC):
                        for t in range(ST):
                            mm = T.transpose(unit(name)[:, k * S + t * P:k * S + (t + 1) * P],
                                             src[:, t, k * P:(k + 1) * P], ident)
                elif name in ("op", "lg"):
                    before, lhs, w, n = ("at", attnT, wo, D) if name == "op" else ("xt", x1T, gw, E)
                    was_emptied(pe, b + LAG[before], before)
                    for t in range(ST):
                        for k in range(KC):
                            mm = T.matmul(unit(name)[:, t * n:(t + 1) * n], lhs[:, k, t * P:(t + 1) * P], w[:, k, :],
                                          start=(k == 0), stop=(k == KC - 1))
                mm.then_inc(filled[name], 1)

            count = ps_max[:, 1, 0, 0:E]

            def early_positions():
                pe.wait_ge(s_chosen, 1)
                pe.wait_ge(s_running, EARLY + 1)
                T.matmul(position_of(0, EARLY), before16[:], chosen16[:, 0:EARLY], start=True, stop=False)
                T.matmul(position_of(0, EARLY), ones16[:], running16[:, 0:EARLY], start=False, stop=True).then_inc(s_pos, 1)
                total = running16[:, EARLY:EARLY + 1]
                T.matmul(position_of(EARLY, TILES), ones16[:], total.to_broadcast([P, TILES - EARLY, E]),
                         start=True, stop=False)
                T.matmul(count, ones16[:], total.rearrange("p t e -> p (t e)"), start=True, stop=False)

            def later_positions():
                pe.wait_ge(s_chosen, 2)
                for t in range(EARLY, TILES):
                    mm = T.matmul(count, ones16[:], chosen16[:, t, :], start=False, stop=(t == TILES - 1))
                mm.then_inc(s_pos, 1)
                for t in range(EARLY, TILES - 1):
                    T.matmul(position_of(t + 1, TILES), ones16[:],
                             chosen16[:, t:t + 1, :].to_broadcast([P, TILES - t - 1, E]), start=False, stop=False)
                T.matmul(position_of(EARLY, TILES), before16[:], chosen16[:, EARLY:],
                         start=False, stop=True).then_inc(s_pos, 1)

            def body(i, u):
                if isinstance(i, int) and i == 1:
                    pe.wait_ge(s_w, 16 * N_W_DMA)
                    pe.wait_ge(s_const, 16)
                    pe.wait_ge(s_setup, 6)
                    pe.wait_ge(s_setup_pool, 3)
                for step in range(8):
                    units = [name for s, name, lag in UNITS if s == step and runs(i, lag)]
                    lag, pair = (3, step + 2) if step < 6 else (2, step - 6)
                    if runs(i, lag):
                        scores(i - lag, pair, (u + lag) % 2, isinstance(i, int) and i == lag == 2)
                    for n in range(max(2, len(units))):
                        if n < 2 and runs(i, 2):
                            max_scores(i - 2, 2 * step + n, u, isinstance(i, int) and i == 2 and step == 0)
                        if n < len(units):
                            fill(i, u, units[n])
                    if isinstance(i, int) and (i, step) == (B + 3, 3):
                        early_positions()

            pe.wait_ge(s_wqk, 32)
            iterations(pe, body)

            later_positions()
            pe.wait_ge(s_be, 1)
            T.transpose(ps_score[0:1, 1, 0, 0:P], be_f[:, 1:2], ident).then_inc(s_be, 1)
            for t in range(TILES):
                pe.wait_ge(s_ohtok, t + 1)
                if t % OH_TILES == 0:
                    pe.wait_ge(s_oh, t // OH_TILES + 1)
                for k in range(TOPK):
                    mm = T.matmul(ps_unit[:, 0, 0:NBLK], oh_in[:, t, k], oh_blk[:, t, k], start=(t + k == 0),
                                  stop=(t == TILES - 1 and k == TOPK - 1))
            mm.then_inc(s_filled_ids, 1)
            for _ in range(WARM_UP):
                T.matmul(ps_max[:, 1, 1], ident, cst[:, 0:S], start=True, stop=True)

            pe.wait_ge(s_be, 3)
            pe.wait_ge(s_experts, 16 * (len(WGU_AT) + 1))

            TRIP = 16
            loaded = {}

            def expert(b):
                return pe.value_load(be_i[0:1, bass.ds(b, 1)], min_val=0, max_val=(E - 1) * D)

            def blk(k, place):
                full = not isinstance(k, int)
                u8 = place % 8
                if full or 0 <= k - 1 < NBLK:
                    w_up = loaded[place - 1] = expert(k - 1)
                if full or k < NBLK:
                    u = u8 % 2
                    pe.wait_ge(s_xg[u8], 2 * (k - u8) + 16)
                    if full or k >= 2:
                        pe.wait_ge(s_xte, k - 1)
                    for n in range(KC):
                        mm = T.transpose(ps_score[:, 0, 2 * u, n * P:(n + 1) * P], xg[:, u8, n * P:(n + 1) * P], ident)
                    mm.then_inc(s_xt, 1)
                if full or 0 <= k - 1 < NBLK:
                    b, u = k - 1, (u8 - 1) % 2
                    pe.wait_ge(s_xte, b + 1)
                    if full or b >= 2:
                        pe.wait_ge(s_in, b - 1)
                    for n in range(KC):
                        mm = T.matmul(ps_score[:, 1, 2 * u, :], xgT[:, u, n, :],
                                      wgu_flat[:, n, bass.ds(w_up, 2 * I)],
                                      start=(n == 0), stop=(n == KC - 1))
                    mm.then_inc(s_gu, 1)
                if full or 0 <= k - 3 < NBLK:
                    w_down = loaded[place - 3] if place >= 2 and (full or k < NBLK) else expert(k - 3)
                if full or 0 <= k - 2 < NBLK:
                    b, u = k - 2, u8 % 2
                    pe.wait_ge(s_in, b + 1)
                    if full or b >= 2:
                        pe.wait_ge(s_ite, b - 1)
                    T.transpose(ps_max[:, u, 0, 0:P], inter[:, u, :], ident).then_inc(s_it, 1)
                if full or 0 <= k - 3 < NBLK:
                    b, u = k - 3, (u8 - 3) % 2
                    pe.wait_ge(s_ite, b + 1)
                    if full or b >= 2:
                        pe.wait_ge(s_ye, b - 1)
                    T.matmul(ps_unit[:, u, 0:D], interT[:, u, :],
                             wdn_flat[:, bass.ds(w_down, D)],
                             start=True, stop=True).then_inc(s_y, 1)

            for k in range(TRIP):
                blk(k, k)
            with pe.Fori(0, NBLK // TRIP - 1) as trip:
                for place in range(TRIP):
                    blk(TRIP * trip + (TRIP + place), place)
            for k in range(NBLK, NBLK + 3):
                blk(k, k % TRIP)


def constants():
    a = np.zeros((P, NCONST), np.float32)

    def put(name, v):
        lo, hi = CONST[name]
        a[:, lo:hi] = np.asarray(v, np.float32).reshape(-1, hi - lo)

    p = np.arange(P)
    put("ident", np.eye(P))
    put("before", p[:, None] < p[None, :])
    inv_freq = (np.float32(1.0) / np.float32(10000.0) ** (np.arange(0, DH, 2, dtype=np.float32) / np.float32(DH)))
    angle = (np.arange(S, dtype=np.float32)[:, None] * inv_freq.astype(np.float32)).astype(np.float32)
    cos, sin = np.cos(angle), np.sin(angle)
    cos = np.concatenate([cos, cos], 1)
    sin = np.concatenate([-sin, sin], 1)
    for name, v in (("cos", cos), ("sin", sin)):
        v = np.repeat(v.reshape(ST, P, DH, 1), 8, axis=3).transpose(1, 0, 2, 3)
        put(name, v.reshape(P, ST * P))
    put("rev", E - np.arange(E))
    e = np.arange(E)
    put("lower", e[None, :] < e[:, None])
    put("iota", p)
    put("blocks", np.arange(NBLK))
    put("token", P * np.arange(TILES)[None, :] + p[:, None] - ID0)
    return a


def kernel(L0_attn_x, L0_attn_q_w, L0_attn_k_w, L0_attn_v_w, L0_attn_q_b, L0_attn_k_b, L0_attn_v_b,
           L0_attn_out_w, L0_attn_out_b, L0_ffn_gate_w, L0_ffn_gate_up_proj, L0_ffn_down_proj):
    import concourse.bacc as bacc
    from concourse.bass_utils import run_bass_kernel_spmd

    def arr(v):
        return np.ascontiguousarray(v)

    def by_dim(w):
        w = np.asarray(w)
        return w.reshape(2, 8, DH, -1).transpose(0, 2, 1, 3).reshape(w.shape)

    x = np.asarray(L0_attn_x).reshape(TOK, D)
    bqk = np.concatenate([by_dim(L0_attn_q_b), by_dim(L0_attn_k_b)])
    arrays = {
        "x": arr(x),
        "xT": arr(x.T),
        "wqkT": arr(np.concatenate([by_dim(L0_attn_q_w), by_dim(L0_attn_k_w)]).T),
        "wvT": arr(np.asarray(L0_attn_v_w).T),
        "woT": arr(np.asarray(L0_attn_out_w).T),
        "gateT": arr(np.asarray(L0_ffn_gate_w).T),
        "bqk": arr(np.broadcast_to(bqk, (P, 2 * D))),
        "bv": arr(np.broadcast_to(np.asarray(L0_attn_v_b), (P, D))),
        "bo": arr(np.broadcast_to(np.asarray(L0_attn_out_b), (P, D))),
        "gup": arr(L0_ffn_gate_up_proj),
        "down": arr(L0_ffn_down_proj),
        "const": constants(),
    }
    nc = bacc.Bacc("TRN2", target_bir_lowering=False, num_devices=1)
    args = [nc.dram_tensor(f"in_{name}", a.shape, mybir.dt.from_np(a.dtype), kind="ExternalInput").ap()
            for name, a in arrays.items()]
    out = nc.dram_tensor("out", (TOK, D), F32, kind="ExternalOutput").ap()
    build(nc, *args, out)
    r = run_bass_kernel_spmd(nc, [{f"in_{name}": a for name, a in arrays.items()}], core_ids=[0])
    return r.results[0]["out"].reshape(B, S, D)
```
